# Optimizing a Trainium2 kernel written in Bass

```python
import numpy as np
import jax
import jax.numpy as jnp

def _softmax(x, axis=-1):
    return jax.nn.softmax(x, axis=axis)

def _gelu(x):
    return jax.nn.gelu(x, approximate=True)

def _silu(x):
    return jax.nn.silu(x)

def _sigmoid(x):
    return jax.nn.sigmoid(x)

def _layernorm(x, axis=-1, eps=1e-05):
    m = jnp.mean(x, axis=axis, keepdims=True)
    v = jnp.var(x, axis=axis, keepdims=True)
    return (x - m) / jnp.sqrt(v + eps)

def _scatter_add(tgt, idx, src, axis=0):
    return tgt.at[idx].add(src)

def _segment_sum(src, seg, n):
    return jax.ops.segment_sum(src, seg, n)
kernel_name = 'mk_xattn_seq_d2_seqx_r4_361975'

def setup_inputs(seed: int=0):
    np.random.seed(seed)
    _w = jnp.asarray

    def _rec_inputs():
        import jax
        import jax.numpy as jnp
        _rk = jax.random.key(seed)
        x = -0.000125 + 0.9999 * jax.random.normal(jax.random.fold_in(_rk, 1), (32, 256, 256), jnp.float32)
        _lenS = 256 - jax.random.randint(jax.random.fold_in(_rk, 7), (32,), 0, max(1, 256 // 4) + 1, jnp.int32)
        _lenS2 = 256 - jax.random.randint(jax.random.fold_in(_rk, 8), (32,), 0, max(1, 256 // 4) + 1, jnp.int32)
        _ctx_2048P = jax.random.normal(jax.random.fold_in(_rk, 11), (32, 16, 512), jnp.float32)
        _ctx_2048c = jax.random.dirichlet(jax.random.fold_in(_rk, 511), 0.3 * jnp.ones((16,), jnp.float32), (32, 256))
        _ctx_2048t = jnp.einsum('bsk,bkd->bsd', _ctx_2048c, _ctx_2048P)
        _ctx_2048t = _ctx_2048t * jax.lax.rsqrt(jnp.mean(jnp.square(_ctx_2048t)) + 1e-12) * 0.953939
        ctx_2048 = 5.36139e-06 + 1.00015 * (_ctx_2048t + 0.3 * jax.random.normal(jax.random.fold_in(_rk, 611), (32, 256, 512), jnp.float32))
        _validS = jnp.arange(256)[None, :] < _lenS[:, None]
        _validS2 = jnp.arange(256)[None, :] < _lenS2[:, None]
        _causal = jnp.tril(jnp.ones((256, 256), dtype=bool))
        mask_S_fk1 = jnp.where(_validS[0], 1.0, 0.0).astype(jnp.float32)
        mask_S_fk0 = jnp.where(_validS[0], 0.0, 1.0).astype(jnp.float32)
        return (x, ctx_2048, mask_S_fk1, mask_S_fk0)
    x, ctx_2048, mask_S_fk1, mask_S_fk0 = _rec_inputs()

    def _L0_xattn_setup():
        import jax, jax.numpy as jnp
        import numpy as np
        HEADS = 16
        HEAD_DIM = 64
        SUPPRESS = 20.0
        key = jax.random.key(seed)
        ks = jax.random.split(key, 8)
        B, HW, C, T, CT = (8, 1024, 256, 77, 512)
        inner = HEADS * HEAD_DIM
        scale = 0.02
        return {'hidden_states': jax.random.normal(ks[0], (B, HW, C), jnp.float32), 'encoder_hidden_states': jax.random.normal(ks[1], (B, T, CT), jnp.float32), 'mask_A': (jax.random.uniform(ks[2], (HW,)) > 0.5).astype(jnp.float32), 'mask_B': (jax.random.uniform(ks[3], (HW,)) > 0.5).astype(jnp.float32), 'Wq': jax.random.normal(ks[4], (C, inner), jnp.float32) * scale, 'Wk': jax.random.normal(ks[5], (CT, inner), jnp.float32) * scale, 'Wv': jax.random.normal(ks[6], (CT, inner), jnp.float32) * scale, 'Wo': jax.random.normal(ks[7], (inner, C), jnp.float32) * scale, 'bo': jnp.zeros((C,), jnp.float32), 'token_indices_A': jnp.array([2, 3], dtype=jnp.int64), 'token_indices_B': jnp.array([5, 6], dtype=jnp.int64)}
    _L0_xattn_all = _L0_xattn_setup()
    _L0_xattn_in = {k: v for k, v in _L0_xattn_all.items() if k in ('Wq', 'Wk', 'Wv', 'Wo', 'bo', 'token_indices_A', 'token_indices_B')}
    del _L0_xattn_all

    def _L1_xattn_setup():
        import jax, jax.numpy as jnp
        import numpy as np
        HEADS = 16
        HEAD_DIM = 64
        SUPPRESS = 20.0
        key = jax.random.key(seed)
        ks = jax.random.split(key, 8)
        B, HW, C, T, CT = (8, 1024, 256, 77, 512)
        inner = HEADS * HEAD_DIM
        scale = 0.02
        return {'hidden_states': jax.random.normal(ks[0], (B, HW, C), jnp.float32), 'encoder_hidden_states': jax.random.normal(ks[1], (B, T, CT), jnp.float32), 'mask_A': (jax.random.uniform(ks[2], (HW,)) > 0.5).astype(jnp.float32), 'mask_B': (jax.random.uniform(ks[3], (HW,)) > 0.5).astype(jnp.float32), 'Wq': jax.random.normal(ks[4], (C, inner), jnp.float32) * scale, 'Wk': jax.random.normal(ks[5], (CT, inner), jnp.float32) * scale, 'Wv': jax.random.normal(ks[6], (CT, inner), jnp.float32) * scale, 'Wo': jax.random.normal(ks[7], (inner, C), jnp.float32) * scale, 'bo': jnp.zeros((C,), jnp.float32), 'token_indices_A': jnp.array([2, 3], dtype=jnp.int64), 'token_indices_B': jnp.array([5, 6], dtype=jnp.int64)}
    _L1_xattn_all = _L1_xattn_setup()
    _L1_xattn_in = {k: v for k, v in _L1_xattn_all.items() if k in ('Wq', 'Wk', 'Wv', 'Wo', 'bo', 'token_indices_A', 'token_indices_B')}
    del _L1_xattn_all
    return {'x': x, 'ctx_2048': ctx_2048, 'mask_S_fk1': mask_S_fk1, 'mask_S_fk0': mask_S_fk0, 'L0_xattn_Wq': _L0_xattn_in['Wq'], 'L0_xattn_Wk': _L0_xattn_in['Wk'], 'L0_xattn_Wv': _L0_xattn_in['Wv'], 'L0_xattn_Wo': _L0_xattn_in['Wo'], 'L0_xattn_bo': _L0_xattn_in['bo'], 'L0_xattn_token_indices_A': _L0_xattn_in['token_indices_A'], 'L0_xattn_token_indices_B': _L0_xattn_in['token_indices_B'], 'L1_xattn_Wq': _L1_xattn_in['Wq'], 'L1_xattn_Wk': _L1_xattn_in['Wk'], 'L1_xattn_Wv': _L1_xattn_in['Wv'], 'L1_xattn_Wo': _L1_xattn_in['Wo'], 'L1_xattn_bo': _L1_xattn_in['bo'], 'L1_xattn_token_indices_A': _L1_xattn_in['token_indices_A'], 'L1_xattn_token_indices_B': _L1_xattn_in['token_indices_B']}

def reference(x, ctx_2048, mask_S_fk1, mask_S_fk0, L0_xattn_Wq, L0_xattn_Wk, L0_xattn_Wv, L0_xattn_Wo, L0_xattn_bo, L0_xattn_token_indices_A, L0_xattn_token_indices_B, L1_xattn_Wq, L1_xattn_Wk, L1_xattn_Wv, L1_xattn_Wo, L1_xattn_bo, L1_xattn_token_indices_A, L1_xattn_token_indices_B):
    import jax
    import jax.numpy as jnp

    def _L0_xattn_ref(hidden_states, encoder_hidden_states, mask_A, mask_B, Wq, Wk, Wv, Wo, bo, token_indices_A, token_indices_B):
        import jax, jax.numpy as jnp
        import numpy as np
        HEADS = 16
        HEAD_DIM = 64
        SUPPRESS = 20.0
        B, HW, C = hidden_states.shape
        T = encoder_hidden_states.shape[1]
        residual = hidden_states
        q = hidden_states @ Wq
        k = encoder_hidden_states @ Wk
        v = encoder_hidden_states @ Wv
        q = q.reshape(B, HW, HEADS, HEAD_DIM).transpose(0, 2, 1, 3)
        k = k.reshape(B, T, HEADS, HEAD_DIM).transpose(0, 2, 1, 3)
        v = v.reshape(B, T, HEADS, HEAD_DIM).transpose(0, 2, 1, 3)
        scale = HEAD_DIM ** (-0.5)
        logits = jnp.einsum('bhqd,bhkd->bhqk', q, k) * scale
        suppress_A_in = 1.0 - mask_A
        suppress_B_in = 1.0 - mask_B
        col_bias = jnp.zeros((HW, T), logits.dtype)
        col_bias = col_bias.at[:, token_indices_A].set((-SUPPRESS * suppress_A_in)[:, None])
        col_bias = col_bias.at[:, token_indices_B].set((-SUPPRESS * suppress_B_in)[:, None])
        logits = logits + col_bias[None, None, :, :]
        probs = jax.nn.softmax(logits, axis=-1)
        out = jnp.einsum('bhqk,bhkd->bhqd', probs, v)
        out = out.transpose(0, 2, 1, 3).reshape(B, HW, HEADS * HEAD_DIM)
        out = out @ Wo + bo
        out = out + residual
        return out

    def _L1_xattn_ref(hidden_states, encoder_hidden_states, mask_A, mask_B, Wq, Wk, Wv, Wo, bo, token_indices_A, token_indices_B):
        import jax, jax.numpy as jnp
        import numpy as np
        HEADS = 16
        HEAD_DIM = 64
        SUPPRESS = 20.0
        B, HW, C = hidden_states.shape
        T = encoder_hidden_states.shape[1]
        residual = hidden_states
        q = hidden_states @ Wq
        k = encoder_hidden_states @ Wk
        v = encoder_hidden_states @ Wv
        q = q.reshape(B, HW, HEADS, HEAD_DIM).transpose(0, 2, 1, 3)
        k = k.reshape(B, T, HEADS, HEAD_DIM).transpose(0, 2, 1, 3)
        v = v.reshape(B, T, HEADS, HEAD_DIM).transpose(0, 2, 1, 3)
        scale = HEAD_DIM ** (-0.5)
        logits = jnp.einsum('bhqd,bhkd->bhqk', q, k) * scale
        suppress_A_in = 1.0 - mask_A
        suppress_B_in = 1.0 - mask_B
        col_bias = jnp.zeros((HW, T), logits.dtype)
        col_bias = col_bias.at[:, token_indices_A].set((-SUPPRESS * suppress_A_in)[:, None])
        col_bias = col_bias.at[:, token_indices_B].set((-SUPPRESS * suppress_B_in)[:, None])
        logits = logits + col_bias[None, None, :, :]
        probs = jax.nn.softmax(logits, axis=-1)
        out = jnp.einsum('bhqk,bhkd->bhqd', probs, v)
        out = out.transpose(0, 2, 1, 3).reshape(B, HW, HEADS * HEAD_DIM)
        out = out @ Wo + bo
        out = out + residual
        return out
    x = _L0_xattn_ref(x, ctx_2048, mask_S_fk1, mask_S_fk0, L0_xattn_Wq, L0_xattn_Wk, L0_xattn_Wv, L0_xattn_Wo, L0_xattn_bo, L0_xattn_token_indices_A, L0_xattn_token_indices_B)
    x = _L1_xattn_ref(x, ctx_2048, mask_S_fk1, mask_S_fk0, L1_xattn_Wq, L1_xattn_Wk, L1_xattn_Wv, L1_xattn_Wo, L1_xattn_bo, L1_xattn_token_indices_A, L1_xattn_token_indices_B)
    return x

_drawn_inputs = setup_inputs


def setup_inputs(seed=0):
    import zlib

    import numpy as np

    out = dict(_drawn_inputs(seed))
    spreads = {'L0_xattn_bo': (0.0, 0.1), 'L1_xattn_bo': (0.0, 0.1)}
    factors = {'mask_S_fk1': 8.0,
     'mask_S_fk0': 8.0,
     'L0_xattn_Wq': 7.881,
     'L0_xattn_Wk': 7.882,
     'L1_xattn_Wq': 7.759,
     'L1_xattn_Wk': 7.764}
    for name, (base, spread) in spreads.items():
        noise = np.random.default_rng([zlib.crc32(name.encode()), seed]).standard_normal(out[name].shape)
        drawn = base * np.exp(spread * noise) if base else spread * noise
        out[name] = jnp.asarray(drawn.astype(out[name].dtype))
    for name, factor in factors.items():
        out[name] = (out[name] * factor).astype(out[name].dtype)
    return out
```

```python
from contextlib import ExitStack

import concourse.bass as bass
from concourse import mybir

F32 = mybir.dt.float32
F32R = mybir.dt.float32r
I32 = mybir.dt.int32
ALU = mybir.AluOpType
ACT = mybir.ActivationFunctionType

P = 128
SEQ = 256
CH = 256
CTX = 512
HEADS = 16
HD = 64
INNER = HEADS * HD
SCALE = HD ** -0.5
SUPPRESS = 20.0
BATCHES = 32
LAYERS = 2

GB = 2
TOK = GB * SEQ
GROUPS = BATCHES // GB
TT = TOK // P
CT = CTX // P
XT = CH // P
QT = SEQ // P
KT = SEQ // P
PAIRS = HEADS // 2
UNITS = PAIRS * GB
QUADS = HEADS // 4
FMAX = 3.4028234e38

CHUNKS = [("k", i) for i in range(CT)] + [("q", i) for i in range(XT)] \
    + [("v", i) for i in range(CT)] + [("o", i) for i in range(2)]
STAGES = 4


def slot_jobs(layer, u, more):
    s = u % UNITS
    pair, quad = s // GB, s // 4
    early, late = [], []
    if s % 2 == 0 and (pair + 1 < PAIRS or more):
        early.append(("q", (pair + 1) % PAIRS, 0))
    if s % 2 == 1 and (pair + 2 < PAIRS or more):
        early.append(("k", (pair + 2) % PAIRS, 0))
    if s == 12 and more:
        early += [("ctx", 0, 0), ("ctx", 1, 0)]
        late += [("ctx", 2, 0), ("ctx", 3, 0)]
    if quad + 1 < QUADS or more:
        late.append(("v", (quad + 1) % QUADS, s % 4))
    if s == 13 and more and layer == 0:
        late += [("x", i, 0) for i in range(XT)]
    if u == UNITS + 1 and layer == 1:
        late += [("y", i, 0) for i in range(2)]
    return early, late


def first_jobs(layer):
    before = [("ctx", i, 0) for i in range(CT)]
    if layer == 0:
        before += [("x", i, 0) for i in range(XT)]
    before += [("q", 0, 0), ("k", 0, 0)]
    return before, [("k", 1, 0)] + [("v", 0, t) for t in range(TT)]


def jobs_of_a_group(layer):
    return sum(len(a) + len(b) for a, b in (slot_jobs(layer, u, True) for u in range(2, UNITS + 2)))


def jobs_before(layer, u, more=True):
    n = sum(map(len, first_jobs(layer)))
    n += sum(len(a) + len(b) for a, b in (slot_jobs(layer, v, more or v < 2) for v in range(u)))
    return n


def two_layers_of_cross_attention(nc, x, ctx, mask_a, mask_b, weights, out):
    with ExitStack() as stack:
        def sb(name, shape, dt=F32):
            return stack.enter_context(nc.sbuf_tensor(name, shape, dt))

        def sem(name):
            return stack.enter_context(nc.semaphore(name))

        def per_layer(name):
            return [sem(f"{name}_{n}") for n in range(LAYERS)]

        w_shapes = {"q": [P, XT, INNER], "k": [P, CT, INNER], "v": [P, CT, INNER], "o": [P, PAIRS, CH]}
        w_hi = {k: sb(f"w{k}_hi", s, F32R) for k, s in w_shapes.items()}
        w_lo = {k: sb(f"w{k}_lo", s, F32R) for k, s in w_shapes.items()}
        ctx_raw = sb("ctx_raw", [P, TT, CTX])
        x_raw = sb("x_raw", [P, TT * CH])
        ctx_hi, ctx_lo = (sb(f"ctxT_{n}", [P, CT, TOK], F32R) for n in ("hi", "lo"))
        x_hi, x_lo = (sb(f"xT_{n}", [P, XT, TOK], F32R) for n in ("hi", "lo"))
        q_hi, q_lo = (sb(f"qT_{n}", [P, 2, TOK], F32R) for n in ("hi", "lo"))
        k_hi, k_lo = (sb(f"kT_{n}", [P, 2, TOK], F32R) for n in ("hi", "lo"))
        v_both = sb("v_both", [P, 2, TT, 4, 2 * HD], F32R)
        probs = sb("probs", [P, 4, QT * SEQ])
        neg_max = sb("neg_max", [P, 4 * QT])
        row_sum = sb("row_sum", [P, 4 * QT])
        row_inv = sb("row_inv", [P, 4 * QT])
        pt_hi, pt_lo = (sb(f"probsT_{n}", [P, 2, KT * SEQ], F32R) for n in ("hi", "lo"))
        o_part = sb("o_part", [P, SEQ])
        o_sum = sb("o_sum", [P, SEQ])
        o_hi, o_lo = (sb(f"oT_{n}", [P, 2, TOK], F32R) for n in ("hi", "lo"))
        y_t = sb("y_t", [P, XT, TOK])
        y_rows = sb("y_rows", [P, TT, CH])
        neg_bias = sb("neg_bias", [P, QT, SEQ])
        identity = sb("identity", [P, P])
        bo_col = sb("bo_col", [P, LAYERS * XT])
        mask_col = sb("mask_col", [P, 2 * QT])
        mask_term = sb("mask_term", [P, 2 * QT])
        index_int = sb("index_int", [P, LAYERS * 4], I32)
        index_f = sb("index_f", [P, LAYERS * 4])
        index_wrap = sb("index_wrap", [P, LAYERS * 4])
        column_int = sb("column_int", [P, SEQ], I32)
        column = o_part
        is_a, is_b, is_one = (ctx_raw[:, t, 0:SEQ] for t in range(3))
        stage = [probs[:, 0:2, :].rearrange("p a b -> p (a b)"), probs[:, 2:4, :].rearrange("p a b -> p (a b)"),
                 y_t[:, :, :].rearrange("p a b -> p (a b)"), y_rows[:, :, :].rearrange("p a b -> p (a b)")]

        job_bank = [stack.enter_context(nc.psum_tensor(f"job_bank{i}", [P, 512], F32)) for i in range(2)]
        s_bank = [stack.enter_context(nc.psum_tensor(f"s_bank{i}", [P, QT * SEQ], F32)) for i in range(2)]
        pt_bank = stack.enter_context(nc.psum_tensor("pt_bank", [P, KT * SEQ], F32))
        o_bank = stack.enter_context(nc.psum_tensor("o_bank", [P, 2 * SEQ], F32))
        y_bank = [stack.enter_context(nc.psum_tensor(f"y_bank{i}", [P, TOK], F32)) for i in range(XT)]

        x_mid = nc.dram_tensor("x_mid", [GROUPS, P, XT * TOK], F32, kind="Internal").ap()

        dve_seen = sem("dve_seen")
        pool_seen = sem("pool_seen")
        small_in = sem("small_in")
        pool_setup = sem("pool_setup")
        setup = sem("setup")
        bias_ready = per_layer("bias_ready")
        w_in = [[sem(f"w_in{s}_{n}") for s in range(STAGES)] for n in range(LAYERS)]
        w_hi_done = per_layer("w_hi_done")
        w_lo_done = per_layer("w_lo_done")
        ctx_in = per_layer("ctx_in")
        x_in = per_layer("x_in")
        x_split = per_layer("x_split")
        job_mm = per_layer("job_mm")
        job_hi = per_layer("job_hi")
        job_lo = per_layer("job_lo")
        s_done = per_layer("s_done")
        logits = per_layer("logits")
        exps = per_layer("exps")
        inverse = per_layer("inverse")
        normal = per_layer("normal")
        pt_mm = per_layer("pt_mm")
        pt_hi_done = per_layer("pt_hi_done")
        pt_lo_done = per_layer("pt_lo_done")
        pv_done = per_layer("pv_done")
        o_part_done = per_layer("o_part_done")
        o_sum_done = per_layer("o_sum_done")
        o_hi_done = per_layer("o_hi_done")
        o_lo_done = per_layer("o_lo_done")
        y_mm = per_layer("y_mm")
        y_init = per_layer("y_init")
        y_done = per_layer("y_done")
        y_out = per_layer("y_out")

        def jobs_at(layer, g, u, more=True):
            return g * jobs_of_a_group(layer) + jobs_before(layer, u, more)

        def wait(engine, semaphore, value):
            if not isinstance(value, int) or value > 0:
                engine.wait_ge(semaphore, value)

        LAST = GROUPS - 1
        x_rows = x.rearrange("b s c -> (b s) c").rearrange("(g t p) c -> g p t c", t=TT, p=P)
        ctx_rows = ctx.rearrange("b s c -> (b s) c").rearrange("(g t p) c -> g p t c", t=TT, p=P)
        out_rows = out.rearrange("b s c -> (b s) c").rearrange("(g t p) c -> g p t c", t=TT, p=P)

        block = stack.enter_context(nc.Block())

        @block.sync
        def _(sp):
            def columns(to, of):
                for t in range(of.shape[0] // P):
                    sp.dma_start(to[:, t:t + 1], of[t * P:(t + 1) * P].rearrange("(p a) -> p a", a=1)).then_inc(small_in, 16)

            for i, m in enumerate((mask_a, mask_b)):
                columns(mask_col[:, i * QT:(i + 1) * QT], m)
            for n in range(LAYERS):
                _, _, _, _, bo, at_a, at_b = weights[n]
                columns(bo_col[:, n * XT:(n + 1) * XT], bo)
                for i, at in enumerate((at_a, at_b)):
                    sp.dma_start(index_int[:, 4 * n + 2 * i:4 * n + 2 * i + 2],
                                 at.partition_broadcast(P)).then_inc(small_in, 16)

            for n in range(LAYERS):
                wq, wk, wv, wo = weights[n][:4]

                def load_ctx(g):
                    sp.dma_start(ctx_raw[:, :, :], ctx_rows[g]).then_inc(ctx_in[n], 16)

                def load_x(g):
                    if n == 0:
                        sp.dma_start(x_raw[:, :].rearrange("p (t c) -> p t c", t=TT), x_rows[g]).then_inc(x_in[n], 16)
                    else:
                        sp.dma_start(x_raw[:, :], x_mid[g]).then_inc(x_in[n], 16)

                def store(g, u):
                    if n == 0:
                        sp.wait_ge(y_done[n], g * XT + XT)
                        sp.dma_start(x_mid[g], y_t[:, :, :].rearrange("p a b -> p (a b)")).then_inc(y_out[n], 16)
                    else:
                        sp.wait_ge(job_lo[n], u)
                        sp.dma_start(out_rows[g], y_rows[:, :, :]).then_inc(y_out[n], 16)

                if n == 0:
                    sp.wait_ge(bias_ready[0], 1)
                else:
                    sp.wait_ge(y_mm[0], GROUPS * PAIRS)
                    sp.wait_ge(y_out[0], 16 * GROUPS)
                    sp.sem_inc(y_out[1], 16)
                load_x(0)
                if n == 0:
                    load_ctx(0)
                else:
                    sp.wait_ge(bias_ready[1], 1)
                    load_ctx(0)
                rows = {"q": wq.rearrange("(t p) n -> t p n", p=P), "k": wk.rearrange("(t p) n -> t p n", p=P),
                        "v": wv.rearrange("(t p) n -> t p n", p=P), "o": wo.rearrange("(h j p) c -> h p j c", h=2, p=P)}
                for i, (kind, t) in enumerate(CHUNKS):
                    if i >= STAGES:
                        sp.wait_ge(w_lo_done[n], i - STAGES + 1)
                    to = stage[i % STAGES]
                    if kind == "o":
                        to = to.rearrange("p (j c) -> p j c", j=PAIRS // 2)
                    sp.dma_start(to, rows[kind][t]).then_inc(w_in[n][i % STAGES], 16)
                sp.wait_ge(job_mm[n], CT)
                load_ctx(1)
                if n == 0:
                    sp.wait_ge(job_mm[n], CT + XT)
                else:
                    sp.wait_ge(x_split[n], 2)
                load_x(1)
                with sp.Fori(0, LAST - 1) as g:
                    sp.wait_ge(job_mm[n], jobs_at(n, g, 13))
                    load_ctx(g + 2)
                    if n == 0:
                        sp.wait_ge(job_mm[n], jobs_at(n, g, 14))
                    else:
                        sp.wait_ge(x_split[n], g * 2 + 4)
                    load_x(g + 2)
                    store(g, jobs_at(n, g, UNITS + 2))
                store(LAST - 1, jobs_at(n, LAST - 1, UNITS + 2))
                store(LAST, jobs_at(n, LAST, UNITS, False) + 2)
            sp.wait_ge(y_out[1], 16 * GROUPS + 16)

        @block.gpsimd
        def _(pool):
            pool.memset(identity[:, :], 0.0).then_inc(pool_setup, 1)
            pool.iota(column_int[:, :], pattern=[[1, SEQ]], base=0, channel_multiplier=0).then_inc(pool_setup, 1)
            pool.wait_ge(pool_setup, 2)
            pool.affine_select(out=identity[:, :], in_=identity[:, :], compare_op=ALU.not_equal, fill=1.0,
                               base=0, pattern=[[-1, P]], channel_multiplier=1).then_inc(pool_setup, 1)

            for n in range(LAYERS):
                def normalise(g, h):
                    pool.wait_ge(inverse[n], g * 2 * UNITS + h + 1)
                    pool.sem_inc(pool_seen, 1)
                    for t in range(QT):
                        i = h % 4 * QT + t
                        at = probs[:, h % 4, t * SEQ:(t + 1) * SEQ]
                        last = pool.tensor_scalar(at, at, row_inv[:, i:i + 1], 1.0, ALU.mult, ALU.mult)
                    last.then_inc(normal[n], 1)

                def slot(g, u):
                    normalise(g, 2 * u + 2)
                    normalise(g, 2 * u + 3)

                for h in (0, 1):
                    normalise(0, h)
                for u in range(2):
                    slot(0, u)
                with pool.Fori(0, LAST) as g:
                    for u in range(2, UNITS + 2):
                        slot(g, u)
                for u in range(2, UNITS - 1):
                    slot(LAST, u)

        @block.tensor
        def _(pe):
            pe.wait_ge(pool_setup, 3)
            for n in range(LAYERS):
                def product(to, left, right, first, last):
                    pe.matmul(to, left[0], right[0], start=first, stop=False)
                    pe.matmul(to, left[0], right[1], start=False, stop=False)
                    return pe.matmul(to, left[1], right[0], start=False, stop=last)

                def job(index, kind, i, t, g):
                    bank = job_bank[index_parity(index) % 2]
                    value = index_value(index)
                    if kind in ("q", "k", "v") and i == 0 and t == 0 and kind != "k":
                        wait(pe, job_lo[n], value)
                    else:
                        wait(pe, job_lo[n], value - 1)
                    if kind == "q":
                        if n == 1 and i == 0:
                            pe.wait_ge(x_split[n], g * 2 + 2)
                        for c in range(XT):
                            cols = slice(i * P, (i + 1) * P)
                            mm = product(bank[:, :], (w_hi["q"][:, c, cols], w_lo["q"][:, c, cols]),
                                         (x_hi[:, c, :], x_lo[:, c, :]), c == 0, c == XT - 1)
                    elif kind == "k":
                        for c in range(CT):
                            cols = slice(i * P, (i + 1) * P)
                            mm = product(bank[:, :], (w_hi["k"][:, c, cols], w_lo["k"][:, c, cols]),
                                         (ctx_hi[:, c, :], ctx_lo[:, c, :]), c == 0, c == CT - 1)
                    elif kind == "v":
                        for c in range(CT):
                            rows, cols = slice(t * P, (t + 1) * P), slice(i * 4 * HD, (i + 1) * 4 * HD)
                            mm = product(bank[:, 0:4 * HD], (ctx_hi[:, c, rows], ctx_lo[:, c, rows]),
                                         (w_hi["v"][:, c, cols], w_lo["v"][:, c, cols]), c == 0, c == CT - 1)
                    elif kind == "ctx":
                        if i == 0:
                            pe.wait_ge(ctx_in[n], g * 16 + 16)
                        for r in range(TT):
                            mm = pe.transpose(bank[:, r * P:(r + 1) * P], ctx_raw[:, r, i * P:(i + 1) * P], identity[:, :])
                    elif kind == "x":
                        if i == 0:
                            pe.wait_ge(x_in[n], g * 16 + 16)
                        for r in range(TT):
                            at = r * CH + i * P
                            mm = pe.transpose(bank[:, r * P:(r + 1) * P], x_raw[:, at:at + P], identity[:, :])
                    else:
                        for r in (2 * i, 2 * i + 1):
                            for c in range(XT):
                                at = (r % 2) * CH + c * P
                                mm = pe.transpose(bank[:, at:at + P], y_t[:, c, r * P:(r + 1) * P], identity[:, :])
                    mm.then_inc(job_mm[n], 1)

                def scores(g, u):
                    wait(pe, logits[n], g * 4 * UNITS + 4 * u)
                    slot_of_pair, b = u // GB % 2, u % GB
                    for t in range(QT):
                        for step in range(3):
                            for e in range(2):
                                rows = slice(e * HD, (e + 1) * HD)
                                left = (q_hi, q_hi, q_lo)[step][rows, slot_of_pair, b * SEQ + t * P:b * SEQ + (t + 1) * P]
                                right = (k_hi, k_lo, k_hi)[step][rows, slot_of_pair, b * SEQ:(b + 1) * SEQ]
                                mm = pe.matmul(s_bank[e][:, t * SEQ:(t + 1) * SEQ], left, right,
                                               start=step == 0, stop=step == 2)
                    mm.then_inc(s_done[n], 1)

                def turn(g, h):
                    pe.wait_ge(normal[n], g * 2 * UNITS + h + 1)
                    wait(pe, pt_lo_done[n], g * 2 * UNITS + h)
                    for c in range(KT):
                        for t in range(QT):
                            mm = pe.transpose(pt_bank[:, c * SEQ + t * P:c * SEQ + (t + 1) * P],
                                              probs[:, h % 4, t * SEQ + c * P:t * SEQ + (c + 1) * P], identity[:, :])
                    mm.then_inc(pt_mm[n], 1)

                def times_v(g, u, e):
                    h = 2 * u + e
                    pe.wait_ge(pt_lo_done[n], g * 2 * UNITS + h + 1)
                    if e == 0:
                        wait(pe, o_sum_done[n], g * 2 * UNITS + 2 * u)
                    for c in range(KT):
                        v = v_both[:, u // 4 % 2, u % GB * KT + c, u // GB % 2 * 2 + e, :]
                        for part, first, last in ((pt_hi, c == 0, False), (pt_lo, False, c == KT - 1)):
                            mm = pe.matmul(o_bank[:, e * SEQ:(e + 1) * SEQ], v, part[:, h % 2, c * SEQ:(c + 1) * SEQ],
                                           start=first, stop=last)
                    mm.then_inc(pv_done[n], 1)

                def project_out(g, pair):
                    pe.wait_ge(o_lo_done[n], g * UNITS + 2 * pair + 2)
                    for c in range(XT):
                        cols = slice(c * P, (c + 1) * P)
                        mm = product(y_bank[c][:, :], (w_hi["o"][:, pair, cols], w_lo["o"][:, pair, cols]),
                                     (o_hi[:, pair % 2, :], o_lo[:, pair % 2, :]), pair == 0, pair == PAIRS - 1)
                    mm.then_inc(y_mm[n], 1)

                def slot(g, u, more=True):
                    early, late = slot_jobs(n, u, more)
                    if u % 2 == 1 and (u + 1 < UNITS or more):
                        pe.wait_ge(job_lo[n], jobs_at(n, g, u, more) - len(slot_jobs(n, u - 1, more)[1]))
                    if u + 1 < UNITS or more:
                        scores(g, u + 1)
                    turn(g, 2 * u)
                    for i, (kind, a, b) in enumerate(early):
                        job((jobs_before(n, u, more) + i, g), kind, a, b, g + 1)
                    turn(g, 2 * u + 1)
                    pe.wait_ge(job_lo[n], jobs_at(n, g, u, more))
                    times_v(g, u, 0)
                    if u == UNITS + 1:
                        pe.wait_ge(y_done[n], g * XT + XT)
                    for i, (kind, a, b) in enumerate(late):
                        job((jobs_before(n, u, more) + len(early) + i, g), kind, a, b, g + 1)
                    if u % 2 == 0 and u > 0:
                        project_out(g, u // GB - 1)
                    times_v(g, u, 1)

                def index_value(index):
                    return index[1] * jobs_of_a_group(n) + index[0]

                def index_parity(index):
                    assert jobs_of_a_group(n) % 2 == 0
                    return index[0]

                before, behind = first_jobs(n)
                for i, (kind, a, b) in enumerate(before):
                    if kind == "q":
                        pe.wait_ge(w_lo_done[n], len(CHUNKS))
                    job((i, 0), kind, a, b, 0)
                pe.wait_ge(job_lo[n], len(before))
                scores(0, 0)
                for i, (kind, a, b) in enumerate(behind):
                    job((len(before) + i, 0), kind, a, b, 0)
                for u in range(2):
                    slot(0, u)
                with pe.Fori(0, LAST) as g:
                    for u in range(2, UNITS + 2):
                        slot(g, u)
                for u in range(2, UNITS):
                    slot(LAST, u, more=False)
                project_out(LAST, PAIRS - 1)
                if n == 1:
                    pe.wait_ge(y_done[n], GROUPS * XT)
                    for i in range(2):
                        job((jobs_before(n, UNITS, False) + i, LAST), "y", i, 0, LAST)

        @block.scalar
        def _(act):
            for n in range(LAYERS):
                def high(value, bank, kind, i, t, u, g):
                    act.wait_ge(job_mm[n], value + 1)
                    if kind == "q":
                        ins = act.activation(q_hi[:, i % 2, :], bank[:, :], ACT.Copy, scale=-SCALE)
                    elif kind == "k":
                        ins = act.activation(k_hi[:, i % 2, :], bank[:, :], ACT.Copy)
                    elif kind == "v":
                        ins = act.activation(v_both[:, i % 2, t, :, 0:HD],
                                             bank[:, 0:4 * HD].rearrange("p (h d) -> p h d", h=4), ACT.Copy)
                    elif kind == "ctx":
                        ins = act.activation(ctx_hi[:, i, :], bank[:, :], ACT.Copy)
                    elif kind == "x":
                        ins = act.activation(x_hi[:, i, :], bank[:, :], ACT.Copy)
                    else:
                        if i == 0:
                            act.wait_ge(y_out[n], g * 16 + 16)
                        ins = act.activation(y_rows[:, 2 * i, :], bank[:, 0:CH], ACT.Copy)
                    ins.then_inc(job_hi[n], 1)

                def exponential(g, h):
                    for t in range(QT):
                        act.wait_ge(logits[n], g * 4 * UNITS + 2 * h + t + 1)
                        i = h % 4 * QT + t
                        at = probs[:, h % 4, t * SEQ:(t + 1) * SEQ]
                        act.activation(at, at, ACT.Exp, bias=neg_max[:, i:i + 1], scale=-1.0,
                                       accum_out=row_sum[:, i:i + 1]).then_inc(exps[n], 1)

                def probs_high(g, h):
                    act.wait_ge(pt_mm[n], g * 2 * UNITS + h + 1)
                    act.activation(pt_hi[:, h % 2, :], pt_bank[:, :], ACT.Copy).then_inc(pt_hi_done[n], 1)

                def move_parts(g, u):
                    act.wait_ge(pv_done[n], g * 2 * UNITS + 2 * u + 2)
                    act.activation(o_part[0:HD, :], o_bank[HD:P, 0:SEQ], ACT.Copy).then_inc(o_part_done[n], 1)
                    act.activation(o_part[HD:P, :], o_bank[0:HD, SEQ:2 * SEQ], ACT.Copy).then_inc(o_part_done[n], 1)

                def slot(g, u, more=True):
                    early, late = slot_jobs(n, u, more)
                    if u > 0:
                        move_parts(g, u - 1)
                    probs_high(g, 2 * u)
                    if u + 1 < UNITS or more:
                        exponential(g, 2 * u + 2)
                    for i, (kind, a, b) in enumerate(early):
                        high(jobs_at(n, g, u, more) + i, job_bank[(jobs_before(n, u, more) + i) % 2], kind, a, b, u, g)
                    probs_high(g, 2 * u + 1)
                    if u + 1 < UNITS or more:
                        exponential(g, 2 * u + 3)
                    for i, (kind, a, b) in enumerate(late, len(early)):
                        high(jobs_at(n, g, u, more) + i, job_bank[(jobs_before(n, u, more) + i) % 2], kind, a, b, u, g)

                for i, (kind, t) in enumerate(CHUNKS):
                    act.wait_ge(w_in[n][i % STAGES], 16 * (i // STAGES + 1))
                    to = w_hi[kind][:, t, :] if kind != "o" else w_hi[kind][:, 4 * t:4 * t + 4, :].rearrange("p j c -> p (j c)")
                    act.activation(to, stage[i % STAGES], ACT.Copy).then_inc(w_hi_done[n], 1)
                before, behind = first_jobs(n)
                for i, (kind, a, b) in enumerate(before):
                    high(i, job_bank[i % 2], kind, a, b, 0, 0)
                for h in (0, 1):
                    exponential(0, h)
                for i, (kind, a, b) in enumerate(behind, len(before)):
                    high(i, job_bank[i % 2], kind, a, b, 0, 0)
                for u in range(2):
                    slot(0, u)
                with act.Fori(0, LAST) as g:
                    for u in range(2, UNITS + 2):
                        slot(g, u)
                for u in range(2, UNITS):
                    slot(LAST, u, more=False)
                move_parts(LAST, UNITS - 1)
                if n == 1:
                    done = jobs_before(n, UNITS, False)
                    for i in range(2):
                        high(LAST * jobs_of_a_group(n) + done + i, job_bank[(done + i) % 2], "y", i, 0, UNITS, LAST)

        @block.vector
        def _(dve):
            steps = [0]

            def step(instruction):
                steps[0] += 1
                instruction.then_inc(setup, 1)
                dve.wait_ge(setup, steps[0])

            for n in range(LAYERS):
                def low(value, bank, kind, i, t, g):
                    dve.wait_ge(job_hi[n], value + 1)
                    if kind == "q":
                        ins = dve.scalar_tensor_tensor(out=q_lo[:, i % 2, :], in0=bank[:, :], scalar=-SCALE,
                                                       in1=q_hi[:, i % 2, :].bitcast(F32), op0=ALU.mult, op1=ALU.subtract)
                    elif kind == "k":
                        ins = dve.tensor_tensor(k_lo[:, i % 2, :], bank[:, :], k_hi[:, i % 2, :].bitcast(F32), ALU.subtract)
                    elif kind == "v":
                        ins = dve.tensor_tensor(v_both[:, i % 2, t, :, HD:2 * HD],
                                                bank[:, 0:4 * HD].rearrange("p (h d) -> p h d", h=4),
                                                v_both[:, i % 2, t, :, 0:HD].bitcast(F32), ALU.subtract)
                    elif kind == "ctx":
                        ins = dve.tensor_tensor(ctx_lo[:, i, :], bank[:, :], ctx_hi[:, i, :].bitcast(F32), ALU.subtract)
                    elif kind == "x":
                        ins = dve.tensor_tensor(x_lo[:, i, :], bank[:, :], x_hi[:, i, :].bitcast(F32), ALU.subtract)
                    else:
                        ins = dve.tensor_copy(y_rows[:, 2 * i + 1, :], bank[:, CH:2 * CH])
                    ins.then_inc(job_lo[n], 1)

                def split_x(g):
                    dve.wait_ge(x_in[n], g * 16 + 16)
                    dve.tensor_copy(x_hi[:, :, :].rearrange("p a b -> p (a b)"), x_raw[:, :]).then_inc(x_split[n], 1)
                    dve.wait_ge(x_split[n], g * 2 + 1)
                    dve.tensor_tensor(x_lo[:, :, :].rearrange("p a b -> p (a b)"), x_raw[:, :],
                                      x_hi[:, :, :].rearrange("p a b -> p (a b)").bitcast(F32), ALU.subtract
                                      ).then_inc(x_split[n], 1)

                def begin_y(g):
                    for c in range(XT):
                        dve.scalar_tensor_tensor(out=y_t[:, c, :], in0=x_hi[:, c, :].bitcast(F32),
                                                 scalar=bo_col[:, n * XT + c:n * XT + c + 1],
                                                 in1=x_lo[:, c, :].bitcast(F32), op0=ALU.add, op1=ALU.add).then_inc(y_init[n], 1)

                def end_y(g):
                    dve.wait_ge(y_mm[n], g * PAIRS + PAIRS)
                    dve.wait_ge(y_init[n], g * XT + XT)
                    for c in range(XT):
                        dve.tensor_tensor(y_t[:, c, :], y_bank[c][:, :], y_t[:, c, :], ALU.add).then_inc(y_done[n], 1)

                def logit(g, h):
                    dve.wait_ge(s_done[n], g * UNITS + h // 2 + 1)
                    dve.sem_inc(dve_seen, 1)
                    for t in range(QT):
                        i = h % 4 * QT + t
                        dve.tensor_tensor_reduce(out=probs[:, h % 4, t * SEQ:(t + 1) * SEQ],
                                                 in0=s_bank[h % 2][:, t * SEQ:(t + 1) * SEQ], in1=neg_bias[:, t, :],
                                                 scale=1.0, scalar=FMAX, op0=ALU.add, op1=ALU.min,
                                                 accum_out=neg_max[:, i:i + 1]).then_inc(logits[n], 1)

                def invert(g, h):
                    dve.wait_ge(exps[n], g * 4 * UNITS + 2 * h + 2)
                    i = h % 4 * QT
                    dve.reciprocal(row_inv[:, i:i + QT], row_sum[:, i:i + QT]).then_inc(inverse[n], 1)

                def probs_low(g, h):
                    dve.wait_ge(pt_hi_done[n], g * 2 * UNITS + h + 1)
                    dve.tensor_tensor(pt_lo[:, h % 2, :], pt_bank[:, :], pt_hi[:, h % 2, :].bitcast(F32),
                                      ALU.subtract).then_inc(pt_lo_done[n], 1)

                def sum_parts(g, u):
                    to = slice(u % GB * SEQ, (u % GB + 1) * SEQ)
                    pair = u // GB
                    dve.wait_ge(o_part_done[n], g * 2 * UNITS + 2 * u + 2)
                    wait(dve, o_lo_done[n], g * UNITS + u)
                    for e in range(2):
                        rows = slice(e * HD, (e + 1) * HD)
                        dve.tensor_tensor(o_sum[rows, :], o_bank[rows, e * SEQ:(e + 1) * SEQ], o_part[rows, :],
                                          ALU.add).then_inc(o_sum_done[n], 1)
                    if u % GB == 0 and pair >= 2:
                        dve.wait_ge(y_mm[n], g * PAIRS + pair - 1)
                    dve.wait_ge(o_sum_done[n], g * 2 * UNITS + 2 * u + 2)
                    dve.tensor_copy(o_hi[:, pair % 2, to], o_sum[:, :]).then_inc(o_hi_done[n], 1)
                    dve.wait_ge(o_hi_done[n], g * UNITS + u + 1)
                    dve.tensor_tensor(o_lo[:, pair % 2, to], o_sum[:, :], o_hi[:, pair % 2, to].bitcast(F32),
                                      ALU.subtract).then_inc(o_lo_done[n], 1)

                def slot(g, u, more=True):
                    early, late = slot_jobs(n, u, more)
                    if u > 0:
                        sum_parts(g, u - 1)
                    if u + 1 < UNITS or more:
                        logit(g, 2 * u + 2)
                    probs_low(g, 2 * u)
                    if u + 1 < UNITS or more:
                        logit(g, 2 * u + 3)
                        invert(g, 2 * u + 2)
                    for i, (kind, a, b) in enumerate(early):
                        low(jobs_at(n, g, u, more) + i, job_bank[(jobs_before(n, u, more) + i) % 2], kind, a, b, g)
                    probs_low(g, 2 * u + 1)
                    for i, (kind, a, b) in enumerate(late, len(early)):
                        low(jobs_at(n, g, u, more) + i, job_bank[(jobs_before(n, u, more) + i) % 2], kind, a, b, g)
                    if u + 1 < UNITS or more:
                        invert(g, 2 * u + 3)
                    if u == 13 and more and n == 1:
                        split_x(g + 1)
                    if u == UNITS:
                        end_y(g)
                    if u == UNITS + 1:
                        if n == 0:
                            dve.wait_ge(y_out[n], g * 16 + 16)
                        begin_y(g + 1)

                if n == 0:
                    dve.wait_ge(small_in, 16 * (2 * QT + (XT + 2) * LAYERS))
                    dve.wait_ge(pool_setup, 2)
                    step(dve.tensor_copy(index_f[:, :], index_int[:, :]))
                    step(dve.tensor_scalar(index_wrap[:, :], index_f[:, :], 0.0, float(SEQ), ALU.is_lt, ALU.mult))
                    step(dve.tensor_tensor(index_f[:, :], index_f[:, :], index_wrap[:, :], ALU.add))
                    step(dve.tensor_scalar(mask_term[:, :], mask_col[:, :], -1.0, 1.0, ALU.mult, ALU.add))
                    step(dve.tensor_scalar(mask_term[:, :], mask_term[:, :], SUPPRESS, None, ALU.mult))
                else:
                    dve.wait_ge(y_mm[0], GROUPS * PAIRS)
                step(dve.tensor_copy(column[:, :], column_int[:, :]))
                for i, to in enumerate((is_a, is_b)):
                    at = 4 * n + 2 * i
                    step(dve.tensor_scalar(to, column[:, :], index_f[:, at:at + 1], None, ALU.is_equal))
                    step(dve.tensor_scalar(is_one, column[:, :], index_f[:, at + 1:at + 2], None, ALU.is_equal))
                    step(dve.tensor_tensor(to, to, is_one, ALU.max))
                step(dve.tensor_tensor(is_a, is_a, is_b, ALU.is_gt))
                for t in range(QT):
                    step(dve.tensor_scalar(is_one, is_a, mask_term[:, t:t + 1], None, ALU.mult))
                    step(dve.scalar_tensor_tensor(out=neg_bias[:, t, :], in0=is_b, scalar=mask_term[:, QT + t:QT + t + 1],
                                                  in1=is_one, op0=ALU.mult, op1=ALU.add))
                dve.sem_inc(bias_ready[n], 1)

                for i, (kind, t) in enumerate(CHUNKS):
                    dve.wait_ge(w_hi_done[n], i + 1)
                    part = [w[kind][:, t, :] if kind != "o" else w[kind][:, 4 * t:4 * t + 4, :].rearrange("p j c -> p (j c)")
                            for w in (w_hi, w_lo)]
                    dve.tensor_tensor(part[1], stage[i % STAGES], part[0].bitcast(F32), ALU.subtract).then_inc(w_lo_done[n], 1)
                if n == 1:
                    split_x(0)
                before, behind = first_jobs(n)
                for i, (kind, a, b) in enumerate(before):
                    low(i, job_bank[i % 2], kind, a, b, 0)
                for h in (0, 1):
                    logit(0, h)
                for h in (0, 1):
                    invert(0, h)
                for i, (kind, a, b) in enumerate(behind, len(before)):
                    low(i, job_bank[i % 2], kind, a, b, 0)
                begin_y(0)
                for u in range(2):
                    slot(0, u)
                with dve.Fori(0, LAST) as g:
                    for u in range(2, UNITS + 2):
                        slot(g, u)
                for u in range(2, UNITS):
                    slot(LAST, u, more=False)
                sum_parts(LAST, UNITS - 1)
                end_y(LAST)
                if n == 1:
                    done = jobs_before(n, UNITS, False)
                    for i in range(2):
                        low(LAST * jobs_of_a_group(n) + done + i, job_bank[(done + i) % 2], "y", i, 0, LAST)


_INS = ["x", "ctx_2048", "mask_S_fk1", "mask_S_fk0"] + [
    f"L{n}_xattn_{w}" for n in range(LAYERS)
    for w in ("Wq", "Wk", "Wv", "Wo", "bo", "token_indices_A", "token_indices_B")]


def kernel(**inputs):
    import numpy as _np
    import concourse.bacc as _bacc
    from concourse import mybir as _mybir
    from concourse.bass_utils import run_bass_kernel_spmd as _run

    nc = _bacc.Bacc("TRN2", target_bir_lowering=False, num_devices=1)
    arrays, args = {}, {}
    for name in _INS:
        a = _np.ascontiguousarray(inputs[name])
        arrays[f"in_{name}_dram"] = a
        args[name] = nc.dram_tensor(f"in_{name}_dram", a.shape, _mybir.dt.from_np(a.dtype), kind="ExternalInput").ap()
    out = nc.dram_tensor("out_0_dram", inputs["x"].shape, _mybir.dt.from_np(_np.dtype("float32")), kind="ExternalOutput").ap()
    weights = [[args[f"L{n}_xattn_{w}"] for w in ("Wq", "Wk", "Wv", "Wo", "bo", "token_indices_A", "token_indices_B")]
               for n in range(LAYERS)]
    two_layers_of_cross_attention(nc, args["x"], args["ctx_2048"], args["mask_S_fk1"], args["mask_S_fk0"], weights, out)
    r = _run(nc, [arrays], core_ids=[0])
    return r.results[0]["out_0_dram"]
```

```python
from contextlib import ExitStack

import concourse.bass as bass
from concourse import mybir

F32 = mybir.dt.float32
F32R = mybir.dt.float32r
I32 = mybir.dt.int32
ALU = mybir.AluOpType
ACT = mybir.ActivationFunctionType

P = 128
SEQ = 256
CH = 256
CTX = 512
HEADS = 16
HD = 64
INNER = HEADS * HD
SCALE = HD ** -0.5
SUPPRESS = 20.0
BATCHES = 32
LAYERS = 2

GB = 2
TOK = GB * SEQ
GROUPS = BATCHES // GB
TT = TOK // P
CT = CTX // P
XT = CH // P
QT = SEQ // P
KT = SEQ // P
PAIRS = HEADS // 2
UNITS = PAIRS * GB
QUADS = HEADS // 4
FMAX = 3.4028234e38
PE, ACTIVATION = mybir.EngineType.PE, mybir.EngineType.Activation
VECTOR, POOL = mybir.EngineType.DVE, mybir.EngineType.Pool

CHUNKS = [("k", i) for i in range(CT)] + [("q", i) for i in range(XT)] \
    + [("v", i) for i in range(CT)] + [("o", i) for i in range(2)]
K_Q_CHUNKS = CT + XT
K_Q_V_CHUNKS = K_Q_CHUNKS + CT
STAGES = {0: "P0 P1 Y P0 P1 Y C0 C1 X Y C0 C1".split(), 1: "C0 C1 X C0 C1 X C0 C1 X X C0 C1".split()}
SPLIT_IN_SLOT = {12: (0, 1, 2), 13: (3, 4, 5), 14: (6, 7), 15: (8, 9)}


def chunk_before(layer, i):
    return max((j for j in range(i) if STAGES[layer][j] == STAGES[layer][i]), default=None)


def slot_jobs(layer, u, more):
    s = u % UNITS
    pair, quad = s // GB, s // 4
    places = [[], [], [], []]
    if s % 2 == 0:
        if pair + 1 < PAIRS or more:
            places[1].append(("q", (pair + 1) % PAIRS, 0))
    elif pair + 2 < PAIRS or more:
        places[1].append(("k", (pair + 2) % PAIRS, 0))
    if quad + 1 < QUADS:
        places[1 if s % 2 == 0 else 2].append(("v", quad + 1, s % 4))
    elif more and s == 12:
        places[0].append(("ctx", 0, 0))
        places[2].append(("ctx", 1, 0))
        places[3].append(("ctx", 2, 0))
    elif more and s == 13:
        places[0].append(("ctx", 3, 0))
        if layer == 0:
            places[1].insert(0, ("x", 0, 0))
            places[2].append(("x", 1, 0))
    elif more and s == 14:
        places[1].insert(0, ("v", 0, 0))
        places[3].append(("v", 0, 1))
    elif more:
        places[2].append(("v", 0, 2))
    if u == UNITS:
        places[3].append(("v", 0, 3))
    if u == UNITS + 1 and layer == 1:
        places[3] += [("y", i, 0) for i in range(2)]
    return places


def plan(layer):
    n, last, found = 0, {}, {}

    def number(jobs):
        nonlocal n
        out = []
        for kind, i, t in jobs:
            needs = {"q": "x", "k": "ctx"}.get(kind)
            ready = last[needs] + 1 if i == 0 and needs in last else 0
            out.append((n, kind, i, t, max(n - 1, ready)))
            last[kind] = n
            n += 1
        return out

    turned = [("ctx", i, 0) for i in range(CT)] + [("x", i, 0) for i in range(XT) if layer == 0]
    found["before"] = number(turned + [("q", 0, 0), ("k", 0, 0)])
    found["behind"] = number([("k", 1, 0)] + [("v", 0, t) for t in range(TT)])
    for u in range(UNITS + 2):
        if u == 2:
            start = n
        found["jobs before", u, True] = n
        found[u, True] = [number(place) for place in slot_jobs(layer, u, True)]
    for kind in ("ctx", "x"):
        found[f"{kind} turned"] = max((job[0] + 1 for u in (12, 13) for place in found[u, True] for job in place
                                       if job[1] == kind), default=None)
    found["jobs before", UNITS + 2, True] = n
    found["jobs of a group"] = n - start
    n = start
    for u in range(2, UNITS):
        found["jobs before", u, False] = n
        found[u, False] = [number(place) for place in slot_jobs(layer, u, False)]
    found["end"] = number([("y", i, 0) for i in range(2) if layer == 1])
    found["jobs in all"] = n
    assert found["jobs of a group"] % 2 == 0
    return found


def two_layers_of_cross_attention(nc, x, ctx, mask_a, mask_b, weights, out):
    with ExitStack() as stack:
        def sb(name, shape, dt=F32):
            return stack.enter_context(nc.sbuf_tensor(name, shape, dt))

        def bank(name):
            return stack.enter_context(nc.psum_tensor(name, [P, 512], F32))

        def sem(name):
            return stack.enter_context(nc.semaphore(name))

        def per_layer(name):
            return [sem(f"{name}_{n}") for n in range(LAYERS)]

        w_shapes = {"q": [P, XT, INNER], "k": [P, CT, INNER], "v": [P, CT, INNER], "o": [P, PAIRS, CH]}
        w_hi = {k: sb(f"w{k}_hi", s, F32R) for k, s in w_shapes.items()}
        w_lo = {k: sb(f"w{k}_lo", s, F32R) for k, s in w_shapes.items()}
        ctx_raw = sb("ctx_raw", [P, TT, CTX])
        x_raw = sb("x_raw", [P, TT * CH])
        ctx_hi, ctx_lo = (sb(f"ctxT_{n}", [P, CT, TOK], F32R) for n in ("hi", "lo"))
        x_hi, x_lo = (sb(f"xT_{n}", [P, XT, TOK], F32R) for n in ("hi", "lo"))
        q_both = sb("q_both", [P, 2, 2, TOK], F32R)
        k_dup = sb("k_dup", [P, 2, 2, TOK], F32R)
        k_low = sb("k_low", [P, 2, 2, TOK], F32R)
        v_both = sb("v_both", [P, 2, TT, 4, 2 * HD], F32R)
        probs = sb("probs", [P, 4, QT * SEQ])
        neg_max = sb("neg_max", [P, 4 * QT])
        row_sum = sb("row_sum", [P, 4 * QT])
        row_inv = sb("row_inv", [P, 4 * QT])
        pt_hi, pt_lo = (sb(f"probsT_{n}", [P, 2, KT * SEQ], F32R) for n in ("hi", "lo"))
        o_part = sb("o_part", [P, SEQ])
        o_sum = sb("o_sum", [P, SEQ])
        o_hi, o_lo = (sb(f"oT_{n}", [P, 2, TOK], F32R) for n in ("hi", "lo"))
        y_t = sb("y_t", [P, XT, TOK])
        neg_bias = sb("neg_bias", [P, LAYERS, QT, SEQ])
        identity = sb("identity", [P, P])
        bo_col = sb("bo_col", [P, LAYERS * XT])
        mask_col = sb("mask_col", [P, 2 * QT])
        mask_term = sb("mask_term", [P, 2 * QT])
        index_int = sb("index_int", [P, LAYERS * 4], I32)
        index_f = sb("index_f", [P, LAYERS * 4])
        index_wrap = sb("index_wrap", [P, LAYERS * 4])

        def flat(ap):
            return ap.rearrange("p a b -> p (a b)")

        y_rows = x_raw[:, :].rearrange("p (t c) -> p t c", t=TT)
        stage = {"P0": flat(probs[:, 0:2, :]), "P1": flat(probs[:, 2:4, :]), "Y": flat(y_t[:, :, :]),
                 "C0": flat(ctx_raw[:, 0:2, :]), "C1": flat(ctx_raw[:, 2:4, :]), "X": x_raw[:, :]}

        def chunk(w, i):
            kind, t = CHUNKS[i]
            return w[kind][:, t, :] if kind != "o" else flat(w[kind][:, 4 * t:4 * t + 4, :])

        job_bank = [bank(f"job_bank{i}") for i in range(2)]
        s_bank = [bank(f"s_bank{i}") for i in range(2)]
        pt_bank = bank("pt_bank")
        o_bank = bank("o_bank")
        y_bank = [bank(f"y_bank{i}") for i in range(XT)]
        chosen = pt_bank[:, 0:SEQ]

        x_mid = nc.dram_tensor("x_mid", [GROUPS, P, XT * TOK], F32, kind="Internal").ap()

        dve_seen = sem("dve_seen")
        pool_seen = sem("pool_seen")
        small_in = sem("small_in")
        pool_setup = sem("pool_setup")
        setup = sem("setup")
        w_in = [{s: sem(f"w_in{s}_{n}") for s in sorted(set(STAGES[n]))} for n in range(LAYERS)]
        w_hi_done = per_layer("w_hi_done")
        w_lo_done = per_layer("w_lo_done")
        ctx_in = per_layer("ctx_in")
        x_in = per_layer("x_in")
        x_split = per_layer("x_split")
        job_mm = per_layer("job_mm")
        job_hi = per_layer("job_hi")
        job_lo = per_layer("job_lo")
        k_dup_done = per_layer("k_dup_done")
        s_done = per_layer("s_done")
        logits = per_layer("logits")
        exps = per_layer("exps")
        inverse = per_layer("inverse")
        normal = per_layer("normal")
        pt_mm = per_layer("pt_mm")
        pt_hi_done = per_layer("pt_hi_done")
        pt_lo_done = per_layer("pt_lo_done")
        pv_done = per_layer("pv_done")
        o_part_done = per_layer("o_part_done")
        o_sum_done = per_layer("o_sum_done")
        o_hi_done = per_layer("o_hi_done")
        o_lo_done = per_layer("o_lo_done")
        y_mm = per_layer("y_mm")
        y_init = per_layer("y_init")
        y_done = per_layer("y_done")
        y_out = per_layer("y_out")

        def wait(engine, semaphore, value):
            if not isinstance(value, int) or value > 0:
                engine.wait_ge(semaphore, value)

        LAST = GROUPS - 1
        plans = [plan(n) for n in range(LAYERS)]
        x_rows = x.rearrange("b s c -> (b s) c").rearrange("(g t p) c -> g p t c", t=TT, p=P)
        ctx_rows = ctx.rearrange("b s c -> (b s) c").rearrange("(g t p) c -> g p t c", t=TT, p=P)
        out_rows = out.rearrange("b s c -> (b s) c").rearrange("(g t p) c -> g p t c", t=TT, p=P)

        block = stack.enter_context(nc.Block())

        @block.sync
        def _(sp):
            def columns(to, of):
                for t in range(of.shape[0] // P):
                    sp.dma_start(to[:, t:t + 1], of[t * P:(t + 1) * P].rearrange("(p a) -> p a", a=1)).then_inc(small_in, 16)

            for n in range(LAYERS):
                wq, wk, wv, wo, bo, at_a, at_b = weights[n]
                here = plans[n]
                rows = {"q": wq.rearrange("(t p) n -> t p n", p=P), "k": wk.rearrange("(t p) n -> t p n", p=P),
                        "v": wv.rearrange("(t p) n -> t p n", p=P), "o": wo.rearrange("(h j p) c -> h p j c", h=2, p=P)}

                def load_ctx(g):
                    sp.dma_start(ctx_raw[:, :, :], ctx_rows[g]).then_inc(ctx_in[n], 16)

                def load_x(g):
                    if n == 0:
                        sp.dma_start(x_raw[:, :].rearrange("p (t c) -> p t c", t=TT), x_rows[g]).then_inc(x_in[n], 16)
                    else:
                        sp.dma_start(x_raw[:, :], x_mid[g]).then_inc(x_in[n], 16)

                def load_chunk(i):
                    kind, t = CHUNKS[i]
                    if (before := chunk_before(n, i)) is not None:
                        sp.wait_ge(w_lo_done[n], before + 1)
                    to = stage[STAGES[n][i]]
                    if kind == "o":
                        to = to.rearrange("p (j c) -> p j c", j=PAIRS // 2)
                    sp.dma_start(to, rows[kind][t]).then_inc(w_in[n][STAGES[n][i]], 16)

                def store(g):
                    if n == 0:
                        sp.wait_ge(y_done[n], g * XT + XT)
                        sp.dma_start(x_mid[g], flat(y_t[:, :, :])).then_inc(y_out[n], 16)
                    else:
                        done = here["jobs in all"] if isinstance(g, int) and g == LAST else here["jobs before", UNITS + 2, True]
                        sp.wait_ge(job_lo[n], g * here["jobs of a group"] + done)
                        sp.dma_start(out_rows[g], y_rows).then_inc(y_out[n], 16)

                if n == 0:
                    load_ctx(0)
                    load_x(0)
                    for i, m in enumerate((mask_a, mask_b)):
                        columns(mask_col[:, i * QT:(i + 1) * QT], m)
                    for m in range(LAYERS):
                        columns(bo_col[:, m * XT:(m + 1) * XT], weights[m][4])
                        for i in range(2):
                            sp.dma_start(index_int[:, 4 * m + 2 * i:4 * m + 2 * i + 2],
                                         weights[m][5 + i].partition_broadcast(P)).then_inc(small_in, 16)
                    for i in range(K_Q_CHUNKS):
                        load_chunk(i)
                    sp.wait_ge(job_mm[n], CT + XT)
                    for i in range(K_Q_CHUNKS, len(CHUNKS)):
                        load_chunk(i)
                else:
                    at = (LAST - 1) * plans[0]["jobs of a group"]
                    sp.wait_ge(job_mm[0], at + plans[0]["x turned"])
                    for i in range(K_Q_V_CHUNKS):
                        load_chunk(i)
                        if i == K_Q_V_CHUNKS - 3:
                            sp.wait_ge(w_lo_done[n], i + 1)
                            load_ctx(0)
                    sp.wait_ge(w_lo_done[n], K_Q_V_CHUNKS)
                    sp.wait_ge(y_out[0], 16 * LAST)
                    load_x(0)
                    sp.wait_ge(y_done[0], GROUPS * XT)
                    sp.dma_start(x_mid[LAST], flat(y_t[:, :, :])).then_inc(y_out[0], 16)
                    sp.wait_ge(job_mm[n], CT)
                    for i in range(K_Q_V_CHUNKS, len(CHUNKS)):
                        load_chunk(i)
                    sp.wait_ge(y_out[0], 16 * GROUPS)
                    sp.wait_ge(x_split[n], 2)
                sp.wait_ge(w_lo_done[n], len(CHUNKS))
                load_ctx(1)
                load_x(1)
                with sp.Fori(0, LAST - 1) as g:
                    sp.wait_ge(job_mm[n], g * here["jobs of a group"] + here["ctx turned"])
                    load_ctx(g + 2)
                    if n == 0:
                        sp.wait_ge(job_mm[n], g * here["jobs of a group"] + here["x turned"])
                        load_x(g + 2)
                    store(g)
                    if n == 1:
                        sp.wait_ge(y_out[n], g * 16 + 16)
                        sp.wait_ge(x_split[n], g * 2 + 4)
                        load_x(g + 2)
                store(LAST - 1)

                if n == 1:
                    store(LAST)
                    sp.wait_ge(y_out[1], 16 * GROUPS)

        @block.gpsimd
        def _(pool):
            pool.iota(o_part[:, :].bitcast(I32), pattern=[[1, SEQ]], base=0, channel_multiplier=0).then_inc(pool_setup, 1)
            pool.memset(identity[:, :], 0.0).then_inc(pool_setup, 1)
            pool.wait_ge(pool_setup, 2)
            pool.affine_select(out=identity[:, :], in_=identity[:, :], compare_op=ALU.not_equal, fill=1.0,
                               base=0, pattern=[[-1, P]], channel_multiplier=1).then_inc(pool_setup, 1)
            for e in range(2):
                other = slice((1 - e) * HD, (2 - e) * HD)
                pool.wait_ge(pool_setup, 3 + e)
                pool.memset(k_low[other, :, e, :].bitcast(F32), 0.0).then_inc(pool_setup, 1)

            for n in range(LAYERS):
                here = plans[n]

                def split_output(g, u):
                    to, pair = slice(u % GB * SEQ, (u % GB + 1) * SEQ), u // GB
                    if u % GB == 0 and pair >= 2:
                        pool.wait_ge(y_mm[n], g * PAIRS + pair - 1)
                        pool.sem_inc(pool_seen, 1)
                    pool.wait_ge(o_sum_done[n], g * 2 * UNITS + 2 * u + 2)
                    pool.sem_inc(pool_seen, 1)
                    pool.tensor_scalar(o_hi[:, pair % 2, to], o_sum[:, :], 1.0, 1.0, ALU.mult, ALU.mult).then_inc(o_hi_done[n], 1)
                    pool.wait_ge(o_hi_done[n], g * UNITS + u + 1)
                    pool.tensor_tensor(o_lo[:, pair % 2, to], o_sum[:, :], o_hi[:, pair % 2, to].bitcast(F32),
                                       ALU.subtract).then_inc(o_lo_done[n], 1)

                def normalise(g, h):
                    pool.wait_ge(inverse[n], g * 2 * UNITS + h + 1)
                    pool.sem_inc(pool_seen, 1)
                    for t in range(QT):
                        i = h % 4 * QT + t
                        at = probs[:, h % 4, t * SEQ:(t + 1) * SEQ]
                        last = pool.tensor_scalar(at, at, row_inv[:, i:i + 1], 1.0, ALU.mult, ALU.mult)
                    last.then_inc(normal[n], 1)

                def duplicate(g, pair, place):
                    for index, kind, i, _, _ in place:
                        if kind == "k":
                            pool.wait_ge(job_hi[n], g * here["jobs of a group"] + index + 1)
                            pool.sem_inc(pool_seen, 1)
                            for e in range(2):
                                own, other = slice(e * HD, (e + 1) * HD), slice((1 - e) * HD, (2 - e) * HD)
                                pool.tensor_scalar(k_dup[other, i % 2, e, :], k_dup[own, i % 2, e, :].bitcast(F32),
                                                   1.0, 1.0, ALU.mult, ALU.mult).then_inc(k_dup_done[n], 1)
                                pool.wait_ge(k_dup_done[n], g * 2 * PAIRS + 2 * pair + e + 1)
                                pool.sem_inc(pool_seen, 1)

                def slot(g, u, more=True):
                    if u > 0:
                        split_output(g, u - 1)
                    if u + 1 < UNITS or more:
                        normalise(g, 2 * u + 2)
                        normalise(g, 2 * u + 3)
                    for place in here[u, more]:
                        if any(job[1] == "k" for job in place):
                            pool.wait_ge(normal[n], g * 2 * UNITS + 2 * u + 4)
                            duplicate(g, u // GB + 2, place)

                if n == 0:
                    pool.wait_ge(pool_setup, 5)
                else:
                    pool.wait_ge(o_lo_done[0], GROUPS * UNITS)
                duplicate(0, 0, here["before"])
                for h in (0, 1):
                    normalise(0, h)
                pool.wait_ge(normal[n], 2)
                duplicate(0, 1, here["behind"])
                for u in range(2):
                    slot(0, u)
                with nc.Fori(0, LAST, engines=(POOL,), hint_back_edge=True) as g:
                    for u in range(2, UNITS + 2):
                        slot(g, u)
                for u in range(2, UNITS):
                    slot(LAST, u, more=False)
                split_output(LAST, UNITS - 1)

        @block.tensor
        def _(pe):
            pe.wait_ge(pool_setup, 5)
            for n in range(LAYERS):
                here = plans[n]

                def product(to, left, right, first, last):
                    pe.matmul(to, left[0], right[0], start=first, stop=False)
                    pe.matmul(to, left[0], right[1], start=False, stop=False)
                    return pe.matmul(to, left[1], right[0], start=False, stop=last)

                def jobs(g, place):
                    for index, kind, i, t, ready in place:
                        bank = job_bank[index % 2]
                        wait(pe, job_lo[n], g * here["jobs of a group"] + ready)
                        cols = slice(i * P, (i + 1) * P)
                        if kind == "q":
                            for c in range(XT):
                                mm = product(bank[:, :], (w_hi["q"][:, c, cols], w_lo["q"][:, c, cols]),
                                             (x_hi[:, c, :], x_lo[:, c, :]), c == 0, c == XT - 1)
                        elif kind == "k":
                            for c in range(CT):
                                mm = product(bank[:, :], (w_hi["k"][:, c, cols], w_lo["k"][:, c, cols]),
                                             (ctx_hi[:, c, :], ctx_lo[:, c, :]), c == 0, c == CT - 1)
                        elif kind == "v":
                            rows, cols = slice(t * P, (t + 1) * P), slice(i * 4 * HD, (i + 1) * 4 * HD)
                            for c in range(CT):
                                mm = product(bank[:, 0:4 * HD], (ctx_hi[:, c, rows], ctx_lo[:, c, rows]),
                                             (w_hi["v"][:, c, cols], w_lo["v"][:, c, cols]), c == 0, c == CT - 1)
                        elif kind == "ctx":
                            for r in range(TT):
                                mm = pe.transpose(bank[:, r * P:(r + 1) * P], ctx_raw[:, r, cols], identity[:, :])
                        elif kind == "x":
                            for r in range(TT):
                                at = r * CH + i * P
                                mm = pe.transpose(bank[:, r * P:(r + 1) * P], x_raw[:, at:at + P], identity[:, :])
                        else:
                            for r in (2 * i, 2 * i + 1):
                                for c in range(XT):
                                    at = (r % 2) * CH + c * P
                                    mm = pe.transpose(bank[:, at:at + P], y_t[:, c, r * P:(r + 1) * P], identity[:, :])
                        mm.then_inc(job_mm[n], 1)

                def scores(g, u):
                    wait(pe, logits[n], g * 4 * UNITS + 4 * u)
                    if u % GB == 0:
                        pe.wait_ge(k_dup_done[n], g * 2 * PAIRS + u // GB * 2 + 2)
                    pair, b = u // GB % 2, u % GB
                    for e in range(2):
                        for t in range(QT):
                            q = q_both[:, pair, e, b * SEQ + t * P:b * SEQ + (t + 1) * P]
                            to = s_bank[e][:, t * SEQ:(t + 1) * SEQ]
                            pe.matmul(to, q, k_dup[:, pair, e, b * SEQ:(b + 1) * SEQ], start=True, stop=False)
                            mm = pe.matmul(to, q, k_low[:, pair, e, b * SEQ:(b + 1) * SEQ], start=False, stop=True)
                    mm.then_inc(s_done[n], 1)

                def turn(g, h):
                    pe.wait_ge(normal[n], g * 2 * UNITS + h + 1)
                    wait(pe, pt_lo_done[n], g * 2 * UNITS + h)
                    for c in range(KT):
                        for t in range(QT):
                            mm = pe.transpose(pt_bank[:, c * SEQ + t * P:c * SEQ + (t + 1) * P],
                                              probs[:, h % 4, t * SEQ + c * P:t * SEQ + (c + 1) * P], identity[:, :])
                    mm.then_inc(pt_mm[n], 1)

                def times_v(g, u, e):
                    h = 2 * u + e
                    pe.wait_ge(pt_lo_done[n], g * 2 * UNITS + h + 1)
                    if e == 0:
                        wait(pe, o_sum_done[n], g * 2 * UNITS + 2 * u)
                    for c in range(KT):
                        v = v_both[:, u // 4 % 2, u % GB * KT + c, u // GB % 2 * 2 + e, :]
                        for part, first, last in ((pt_hi, c == 0, False), (pt_lo, False, c == KT - 1)):
                            mm = pe.matmul(o_bank[:, e * SEQ:(e + 1) * SEQ], v, part[:, h % 2, c * SEQ:(c + 1) * SEQ],
                                           start=first, stop=last)
                    mm.then_inc(pv_done[n], 1)

                def project_out(g, pair):
                    pe.wait_ge(o_lo_done[n], g * UNITS + 2 * pair + 2)
                    for c in range(XT):
                        cols = slice(c * P, (c + 1) * P)
                        mm = product(y_bank[c][:, :], (w_hi["o"][:, pair, cols], w_lo["o"][:, pair, cols]),
                                     (o_hi[:, pair % 2, :], o_lo[:, pair % 2, :]), pair == 0, pair == PAIRS - 1)
                    mm.then_inc(y_mm[n], 1)

                def slot(g, u, more=True):
                    places = here[u, more]
                    if u + 1 < UNITS or more:
                        if u % 2 == 1:
                            index = max(j[0] for place in here[u - 1, more] for j in place if j[1] == "q")
                            pe.wait_ge(job_lo[n], g * here["jobs of a group"] + index + 1)
                        scores(g, u + 1)
                    if u == 12 and more:
                        pe.wait_ge(ctx_in[n], g * 16 + 32)
                    if u == 13 and more and n == 0:
                        pe.wait_ge(x_in[n], g * 16 + 32)
                    jobs(g, places[0])
                    turn(g, 2 * u)
                    if u == 14 and more and n == 1:
                        pe.wait_ge(x_split[n], g * 2 + 4)
                    jobs(g, places[1])
                    turn(g, 2 * u + 1)
                    pe.wait_ge(job_lo[n], g * here["jobs of a group"] + here["jobs before", u, more])
                    times_v(g, u, 0)
                    jobs(g, places[2])
                    if u % 2 == 0 and u > 0:
                        project_out(g, u // GB - 1)
                    if u < UNITS + 1:
                        jobs(g, places[3])
                        times_v(g, u, 1)
                    else:
                        times_v(g, u, 1)
                        pe.wait_ge(y_done[n], g * XT + XT)
                        jobs(g, places[3])

                pe.wait_ge(ctx_in[n], 16)
                if n == 0:
                    pe.wait_ge(x_in[n], 16)
                jobs(0, here["before"][:-2])
                pe.wait_ge(w_lo_done[n], K_Q_CHUNKS)
                if n == 1:
                    pe.wait_ge(x_split[n], 2)
                jobs(0, here["before"][-2:])
                pe.wait_ge(job_lo[n], len(here["before"]))
                scores(0, 0)
                pe.wait_ge(w_lo_done[n], K_Q_V_CHUNKS)
                jobs(0, here["behind"])
                for u in range(2):
                    slot(0, u)
                pe.wait_ge(w_lo_done[n], len(CHUNKS))
                with nc.Fori(0, LAST, engines=(PE,), hint_back_edge=True) as g:
                    for u in range(2, UNITS + 2):
                        slot(g, u)
                for u in range(2, UNITS):
                    slot(LAST, u, more=False)
                project_out(LAST, PAIRS - 1)
                if n == 1:
                    pe.wait_ge(y_done[n], GROUPS * XT)
                    jobs(LAST, here["end"])

        @block.scalar
        def _(act):
            def split_chunk(n, i):
                loads = STAGES[n][:i + 1].count(STAGES[n][i])
                act.wait_ge(w_in[n][STAGES[n][i]], 16 * loads)
                act.activation(chunk(w_hi, i), stage[STAGES[n][i]], ACT.Copy).then_inc(w_hi_done[n], 1)

            for n in range(LAYERS):
                here = plans[n]

                def high(g, place):
                    for index, kind, i, t, _ in place:
                        bank = job_bank[index % 2]
                        act.wait_ge(job_mm[n], g * here["jobs of a group"] + index + 1)
                        if kind == "q":
                            for e in range(2):
                                own = slice(e * HD, (e + 1) * HD)
                                ins = act.activation(q_both[own, i % 2, e, :], bank[own, :], ACT.Copy, scale=-SCALE)
                        elif kind == "k":
                            for e in range(2):
                                own = slice(e * HD, (e + 1) * HD)
                                ins = act.activation(k_dup[own, i % 2, e, :], bank[own, :], ACT.Copy)
                        elif kind == "v":
                            ins = act.activation(v_both[:, i % 2, t, :, 0:HD],
                                                 bank[:, 0:4 * HD].rearrange("p (h d) -> p h d", h=4), ACT.Copy)
                        elif kind == "ctx":
                            ins = act.activation(ctx_hi[:, i, :], bank[:, :], ACT.Copy)
                        elif kind == "x":
                            ins = act.activation(x_hi[:, i, :], bank[:, :], ACT.Copy)
                        else:
                            ins = act.activation(y_rows[:, 2 * i, :], bank[:, 0:CH], ACT.Copy)
                        ins.then_inc(job_hi[n], 1)

                def split_x(g):
                    act.wait_ge(x_in[n], g * 16 + 16)
                    act.activation(flat(x_hi[:, :, :]), x_raw[:, :], ACT.Copy).then_inc(x_split[n], 1)

                def exponential(g, h):
                    for t in range(QT):
                        act.wait_ge(logits[n], g * 4 * UNITS + 2 * h + t + 1)
                        i = h % 4 * QT + t
                        at = probs[:, h % 4, t * SEQ:(t + 1) * SEQ]
                        act.activation(at, at, ACT.Exp, bias=neg_max[:, i:i + 1], scale=-1.0,
                                       accum_out=row_sum[:, i:i + 1]).then_inc(exps[n], 1)

                def probs_high(g, h):
                    act.wait_ge(pt_mm[n], g * 2 * UNITS + h + 1)
                    act.activation(pt_hi[:, h % 2, :], pt_bank[:, :], ACT.Copy).then_inc(pt_hi_done[n], 1)

                def move_parts(g, u):
                    act.wait_ge(pv_done[n], g * 2 * UNITS + 2 * u + 2)
                    act.activation(o_part[0:HD, :], o_bank[HD:P, 0:SEQ], ACT.Copy).then_inc(o_part_done[n], 1)
                    act.activation(o_part[HD:P, :], o_bank[0:HD, SEQ:2 * SEQ], ACT.Copy).then_inc(o_part_done[n], 1)

                def slot(g, u, more=True):
                    places = here[u, more]
                    if u > 0:
                        move_parts(g, u - 1)
                    high(g, places[0])
                    probs_high(g, 2 * u)
                    if u + 1 < UNITS or more:
                        exponential(g, 2 * u + 2)
                    if u % 2 == 1:
                        high(g, places[1][:-1])
                        if u + 1 < UNITS or more:
                            exponential(g, 2 * u + 3)
                        probs_high(g, 2 * u + 1)
                        high(g, places[1][-1:])
                    else:
                        high(g, places[1][:1])
                        probs_high(g, 2 * u + 1)
                        high(g, places[1][1:])
                        if u + 1 < UNITS or more:
                            exponential(g, 2 * u + 3)
                    high(g, places[2])
                    high(g, places[3])
                    if u == 12 and more and n == 1:
                        act.wait_ge(y_init[n], g * XT + XT)
                        split_x(g + 1)
                    if n == 0 and not more:
                        for i in SPLIT_IN_SLOT.get(u, ()):
                            split_chunk(1, i)

                high(0, here["before"][:-2])
                if n == 0:
                    for i in range(K_Q_CHUNKS):
                        split_chunk(0, i)
                else:
                    act.wait_ge(y_init[0], GROUPS * XT)
                    split_x(0)
                high(0, here["before"][-2:])
                for h in (0, 1):
                    exponential(0, h)
                if n == 0:
                    for i in range(K_Q_CHUNKS, K_Q_V_CHUNKS):
                        split_chunk(0, i)
                high(0, here["behind"])
                if n == 1:
                    act.wait_ge(y_mm[0], GROUPS * PAIRS)
                for i in range(K_Q_V_CHUNKS, len(CHUNKS)):
                    split_chunk(n, i)
                for u in range(2):
                    slot(0, u)
                with nc.Fori(0, LAST, engines=(ACTIVATION,), hint_back_edge=True) as g:
                    for u in range(2, UNITS + 2):
                        slot(g, u)
                for u in range(2, UNITS):
                    slot(LAST, u, more=False)
                move_parts(LAST, UNITS - 1)
                if n == 1:
                    act.wait_ge(y_out[n], 16 * LAST)
                high(LAST, here["end"])

        @block.vector
        def _(dve):
            def split_chunk(n, i):
                dve.wait_ge(w_hi_done[n], i + 1)
                dve.tensor_tensor(chunk(w_lo, i), stage[STAGES[n][i]], chunk(w_hi, i).bitcast(F32),
                                  ALU.subtract).then_inc(w_lo_done[n], 1)

            steps = [0]

            def step(instruction):
                steps[0] += 1
                instruction.then_inc(setup, 1)
                dve.wait_ge(setup, steps[0])

            dve.wait_ge(small_in, 16 * (2 * QT + (XT + 2) * LAYERS))
            dve.wait_ge(pool_setup, 1)
            step(dve.tensor_copy(o_sum[:, :], o_part[:, :].bitcast(I32)))
            step(dve.tensor_copy(index_f[:, :], index_int[:, :]))
            step(dve.tensor_scalar(index_wrap[:, :], index_f[:, :], 0.0, float(SEQ), ALU.is_lt, ALU.mult))
            step(dve.tensor_tensor(index_f[:, :], index_f[:, :], index_wrap[:, :], ALU.add))
            step(dve.tensor_scalar(mask_term[:, :], mask_col[:, :], -1.0, 1.0, ALU.mult, ALU.add))
            step(dve.tensor_scalar(mask_term[:, :], mask_term[:, :], SUPPRESS, None, ALU.mult))
            for n in range(LAYERS):
                is_a, is_b = neg_bias[:, n, 0, :], neg_bias[:, n, 1, :]
                for i, to in enumerate((is_a, is_b)):
                    at = 4 * n + 2 * i
                    step(dve.tensor_scalar(to, o_sum[:, :], index_f[:, at:at + 1], None, ALU.is_equal))
                    step(dve.tensor_scalar(chosen, o_sum[:, :], index_f[:, at + 1:at + 2], None, ALU.is_equal))
                    step(dve.tensor_tensor(to, chosen, to, ALU.max))
                step(dve.tensor_tensor(is_a, is_a, is_b, ALU.is_gt))
                step(dve.tensor_scalar(chosen, is_a, mask_term[:, 0:1], None, ALU.mult))
                step(dve.scalar_tensor_tensor(out=chosen, in0=is_b, scalar=mask_term[:, QT:QT + 1], in1=chosen,
                                              op0=ALU.mult, op1=ALU.add))
                step(dve.tensor_scalar(is_a, is_a, mask_term[:, 1:2], None, ALU.mult))
                step(dve.scalar_tensor_tensor(out=is_b, in0=is_b, scalar=mask_term[:, QT + 1:QT + 2], in1=is_a,
                                              op0=ALU.mult, op1=ALU.add))
                step(dve.tensor_copy(is_a, chosen))

            for n in range(LAYERS):
                here = plans[n]

                def low(g, place):
                    for index, kind, i, t, _ in place:
                        bank = job_bank[index % 2]
                        dve.wait_ge(job_hi[n], g * here["jobs of a group"] + index + 1)
                        if kind == "q":
                            for e in range(2):
                                own, other = slice(e * HD, (e + 1) * HD), slice((1 - e) * HD, (2 - e) * HD)
                                ins = dve.scalar_tensor_tensor(out=q_both[other, i % 2, e, :], in0=bank[own, :], scalar=-SCALE,
                                                               in1=q_both[own, i % 2, e, :].bitcast(F32),
                                                               op0=ALU.mult, op1=ALU.subtract)
                        elif kind == "k":
                            for e in range(2):
                                own = slice(e * HD, (e + 1) * HD)
                                ins = dve.tensor_tensor(k_low[own, i % 2, e, :], bank[own, :],
                                                        k_dup[own, i % 2, e, :].bitcast(F32), ALU.subtract)
                        elif kind == "v":
                            ins = dve.tensor_tensor(v_both[:, i % 2, t, :, HD:2 * HD],
                                                    bank[:, 0:4 * HD].rearrange("p (h d) -> p h d", h=4),
                                                    v_both[:, i % 2, t, :, 0:HD].bitcast(F32), ALU.subtract)
                        elif kind == "ctx":
                            ins = dve.tensor_tensor(ctx_lo[:, i, :], bank[:, :], ctx_hi[:, i, :].bitcast(F32), ALU.subtract)
                        elif kind == "x":
                            ins = dve.tensor_tensor(x_lo[:, i, :], bank[:, :], x_hi[:, i, :].bitcast(F32), ALU.subtract)
                        else:
                            ins = dve.tensor_copy(y_rows[:, 2 * i + 1, :], bank[:, CH:2 * CH])
                        ins.then_inc(job_lo[n], 1)

                def split_x(g):
                    dve.wait_ge(x_split[n], g * 2 + 1)
                    dve.tensor_tensor(flat(x_lo[:, :, :]), x_raw[:, :], flat(x_hi[:, :, :]).bitcast(F32),
                                      ALU.subtract).then_inc(x_split[n], 1)

                def begin_y(g, c):
                    dve.scalar_tensor_tensor(out=y_t[:, c, :], in0=x_hi[:, c, :].bitcast(F32),
                                             scalar=bo_col[:, n * XT + c:n * XT + c + 1],
                                             in1=x_lo[:, c, :].bitcast(F32), op0=ALU.add, op1=ALU.add).then_inc(y_init[n], 1)

                def end_y(g):
                    dve.wait_ge(y_mm[n], g * PAIRS + PAIRS)
                    dve.wait_ge(y_init[n], g * XT + XT)
                    for c in range(XT):
                        dve.tensor_tensor(y_t[:, c, :], y_bank[c][:, :], y_t[:, c, :], ALU.add).then_inc(y_done[n], 1)

                def logit(g, h):
                    dve.wait_ge(s_done[n], g * UNITS + h // 2 + 1)
                    dve.sem_inc(dve_seen, 1)
                    for t in range(QT):
                        i = h % 4 * QT + t
                        dve.tensor_tensor_reduce(out=probs[:, h % 4, t * SEQ:(t + 1) * SEQ],
                                                 in0=s_bank[h % 2][:, t * SEQ:(t + 1) * SEQ], in1=neg_bias[:, n, t, :],
                                                 scale=1.0, scalar=FMAX, op0=ALU.add, op1=ALU.min,
                                                 accum_out=neg_max[:, i:i + 1]).then_inc(logits[n], 1)

                def invert(g, h):
                    dve.wait_ge(exps[n], g * 4 * UNITS + 2 * h + 2)
                    i = h % 4 * QT
                    dve.reciprocal(row_inv[:, i:i + QT], row_sum[:, i:i + QT]).then_inc(inverse[n], 1)

                def probs_low(g, h):
                    dve.wait_ge(pt_hi_done[n], g * 2 * UNITS + h + 1)
                    dve.tensor_tensor(pt_lo[:, h % 2, :], pt_bank[:, :], pt_hi[:, h % 2, :].bitcast(F32),
                                      ALU.subtract).then_inc(pt_lo_done[n], 1)

                def sum_parts(g, u):
                    dve.wait_ge(o_part_done[n], g * 2 * UNITS + 2 * u + 2)
                    wait(dve, o_lo_done[n], g * UNITS + u)
                    for e in range(2):
                        rows = slice(e * HD, (e + 1) * HD)
                        dve.tensor_tensor(o_sum[rows, :], o_bank[rows, e * SEQ:(e + 1) * SEQ], o_part[rows, :],
                                          ALU.add).then_inc(o_sum_done[n], 1)

                def slot(g, u, more=True):
                    places = here[u, more]
                    if u + 1 < UNITS or more:
                        logit(g, 2 * u + 2)
                    if u % 2 == 1:
                        low(g, places[0])
                    if u > 0:
                        sum_parts(g, u - 1)
                    probs_low(g, 2 * u)
                    if u % 2 == 0:
                        low(g, places[0])
                    if u % 2 == 1:
                        low(g, places[1][:-1])
                    if u + 1 < UNITS or more:
                        logit(g, 2 * u + 3)
                        invert(g, 2 * u + 2)
                    if u % 2 == 1:
                        if u + 1 < UNITS or more:
                            invert(g, 2 * u + 3)
                        probs_low(g, 2 * u + 1)
                        low(g, places[1][-1:])
                    else:
                        low(g, places[1][:1])
                        probs_low(g, 2 * u + 1)
                        low(g, places[1][1:])
                        if u + 1 < UNITS or more:
                            invert(g, 2 * u + 3)
                    low(g, places[2] + places[3])
                    if u == 13 and more and n == 1:
                        split_x(g + 1)
                    if u == UNITS:
                        end_y(g)
                    if u == UNITS + 1 and n == 0:
                        dve.wait_ge(y_out[n], g * 16 + 16)
                    if u in (2, 4):
                        begin_y(g, u // 2 - 1)
                    if n == 0 and not more:
                        for i in SPLIT_IN_SLOT.get(u, ()):
                            split_chunk(1, i)

                low(0, here["before"][:-2])
                if n == 0:
                    for i in range(K_Q_CHUNKS):
                        split_chunk(0, i)
                else:
                    split_x(0)
                low(0, here["before"][-2:])
                for h in (0, 1):
                    logit(0, h)
                if n == 0:
                    for i in range(K_Q_CHUNKS, K_Q_V_CHUNKS):
                        split_chunk(0, i)
                for h in (0, 1):
                    invert(0, h)
                low(0, here["behind"])
                for i in range(K_Q_V_CHUNKS, len(CHUNKS)):
                    split_chunk(n, i)
                for u in range(2):
                    slot(0, u)
                if n == 1:
                    dve.wait_ge(y_out[0], 16 * GROUPS)
                with nc.Fori(0, LAST, engines=(VECTOR,), hint_back_edge=True) as g:
                    for u in range(2, UNITS + 2):
                        slot(g, u)
                for u in range(2, UNITS):
                    slot(LAST, u, more=False)
                sum_parts(LAST, UNITS - 1)
                end_y(LAST)
                if n == 1:
                    dve.wait_ge(y_out[n], 16 * LAST)
                low(LAST, here["end"])


_INS = ["x", "ctx_2048", "mask_S_fk1", "mask_S_fk0"] + [
    f"L{n}_xattn_{w}" for n in range(LAYERS)
    for w in ("Wq", "Wk", "Wv", "Wo", "bo", "token_indices_A", "token_indices_B")]


def kernel(**inputs):
    import numpy as _np
    import concourse.bacc as _bacc
    from concourse import mybir as _mybir
    from concourse.bass_utils import run_bass_kernel_spmd as _run

    nc = _bacc.Bacc("TRN2", target_bir_lowering=False, num_devices=1)
    arrays, args = {}, {}
    for name in _INS:
        a = _np.ascontiguousarray(inputs[name])
        arrays[f"in_{name}_dram"] = a
        args[name] = nc.dram_tensor(f"in_{name}_dram", a.shape, _mybir.dt.from_np(a.dtype), kind="ExternalInput").ap()
    out = nc.dram_tensor("out_0_dram", inputs["x"].shape, _mybir.dt.from_np(_np.dtype("float32")), kind="ExternalOutput").ap()
    weights = [[args[f"L{n}_xattn_{w}"] for w in ("Wq", "Wk", "Wv", "Wo", "bo", "token_indices_A", "token_indices_B")]
               for n in range(LAYERS)]
    two_layers_of_cross_attention(nc, args["x"], args["ctx_2048"], args["mask_S_fk1"], args["mask_S_fk0"], weights, out)
    r = _run(nc, [arrays], core_ids=[0])
    return r.results[0]["out_0_dram"]
```

```python
from contextlib import ExitStack

import concourse.bass as bass
from concourse import mybir

F32 = mybir.dt.float32
F32R = mybir.dt.float32r
I32 = mybir.dt.int32
ALU = mybir.AluOpType
ACT = mybir.ActivationFunctionType

P = 128
SEQ = 256
CH = 256
CTX = 512
HEADS = 16
HD = 64
INNER = HEADS * HD
SCALE = HD ** -0.5
SUPPRESS = 20.0
BATCHES = 32
LAYERS = 2

GB = 2
TOK = GB * SEQ
GROUPS = BATCHES // GB
TT = TOK // P
CT = CTX // P
XT = CH // P
QT = SEQ // P
KT = SEQ // P
PAIRS = HEADS // 2
UNITS = PAIRS * GB
QUADS = HEADS // 4
FMAX = 3.4028234e38
PE, ACTIVATION = mybir.EngineType.PE, mybir.EngineType.Activation
VECTOR, POOL = mybir.EngineType.DVE, mybir.EngineType.Pool

BIAS_FOUND = 11
BIAS_STEPS = 20

CHUNKS = [("k", i) for i in range(CT)] + [("q", i) for i in range(XT)] \
    + [("v", i) for i in range(CT)] + [("o", i) for i in range(2)]
K_Q_CHUNKS = CT + XT
K_Q_V_CHUNKS = K_Q_CHUNKS + CT
STAGES = {0: "P0 P1 Y C0 C1 X P0 P1 Y C0 C1 X".split(), 1: "C0 C1 X C0 C1 X C0 C1 X C0 C1 X".split()}
SPLIT_IN_SLOT = {12: (0, 1, 2), 13: (3, 4, 5), 14: (6, 7, 8), 15: (9,)}


def chunk_before(layer, i):
    return max((j for j in range(i) if STAGES[layer][j] == STAGES[layer][i]), default=None)


def slot_jobs(layer, u, more):
    s = u % UNITS
    pair, quad = s // GB, s // 4
    places = [[], [], [], []]
    if s % 2 == 0:
        if pair + 1 < PAIRS or more:
            places[1].append(("q", (pair + 1) % PAIRS, 0))
    elif pair + 2 < PAIRS or more:
        places[1].append(("k", (pair + 2) % PAIRS, 0))
    if quad + 1 < QUADS:
        places[1 if s % 2 == 0 else 2].append(("v", quad + 1, s % 4))
    elif more and s == 12:
        places[0].append(("ctx", 0, 0))
        places[1].append(("ctx", 1, 0))
        places[3] += [("ctx", i, 0) for i in (2, 3)]
    elif more and s == 13:
        if layer == 0:
            places[1].insert(0, ("x", 0, 0))
        places[2].append(("v", 0, 0))
    elif more and s == 14:
        if layer == 0:
            places[0].append(("x", 1, 0))
        places[1].insert(0, ("v", 0, 1))
        places[3].append(("v", 0, 2))
    elif more:
        places[2].append(("v", 0, 3))
    if u == UNITS + 1 and layer == 1:
        places[0].append(("y", 0, 0))
        places[1].insert(0, ("y", 1, 0))
    return places


def only_k(place):
    return [job[1] for job in place] == ["k"]


def plan(layer):
    n, last, found = 0, {}, {}

    def number(jobs):
        nonlocal n
        out = []
        for kind, i, t in jobs:
            needs = {"q": "x", "k": "ctx"}.get(kind)
            ready = last[needs] + 1 if i == 0 and needs in last else 0
            out.append((n, kind, i, t, max(n - 1, ready)))
            last[kind] = n
            n += 1
        return out

    turned = [("ctx", i, 0) for i in range(CT)] + [("x", i, 0) for i in range(XT) if layer == 0]
    found["before"] = number(turned + [("q", 0, 0), ("k", 0, 0), ("k", 1, 0)])
    found["behind"] = number([("v", 0, t) for t in range(TT)])
    for u in range(UNITS + 2):
        if u == 2:
            start = n
        found["jobs before", u, True] = n
        found[u, True] = [number(place) for place in slot_jobs(layer, u, True)]
    for kind in ("ctx", "x"):
        found[f"{kind} turned"] = max((job[0] + 1 for u in (12, 13, 14) for place in found[u, True] for job in place
                                       if job[1] == kind), default=None)
    found["jobs before", UNITS + 2, True] = n
    found["jobs of a group"] = n - start
    n = start
    for u in range(2, UNITS):
        found["jobs before", u, False] = n
        found[u, False] = [number(place) for place in slot_jobs(layer, u, False)]
    found["end"] = number([("y", i, 0) for i in range(2) if layer == 1])
    found["jobs in all"] = n
    assert found["jobs of a group"] % 2 == 0
    return found


def two_layers_of_cross_attention(nc, x, ctx, mask_a, mask_b, weights, out):
    with ExitStack() as stack:
        def sb(name, shape, dt=F32):
            return stack.enter_context(nc.sbuf_tensor(name, shape, dt))

        def bank(name):
            return stack.enter_context(nc.psum_tensor(name, [P, 512], F32))

        def sem(name):
            return stack.enter_context(nc.semaphore(name))

        def per_layer(name):
            return [sem(f"{name}_{n}") for n in range(LAYERS)]

        w_shapes = {"q": [P, XT, INNER], "k": [P, CT, INNER], "v": [P, CT, INNER], "o": [P, PAIRS, CH]}
        w_hi = {k: sb(f"w{k}_hi", s, F32R) for k, s in w_shapes.items()}
        w_lo = {k: sb(f"w{k}_lo", s, F32R) for k, s in w_shapes.items()}
        ctx_raw = sb("ctx_raw", [P, TT, CTX])
        x_raw = sb("x_raw", [P, TT * CH])
        ctx_hi, ctx_lo = (sb(f"ctxT_{n}", [P, CT, TOK], F32R) for n in ("hi", "lo"))
        x_hi, x_lo = (sb(f"xT_{n}", [P, XT, TOK], F32R) for n in ("hi", "lo"))
        q_both = sb("q_both", [P, 2, 2, TOK], F32R)
        k_dup = sb("k_dup", [P, 2, 2, TOK], F32R)
        k_low = sb("k_low", [P, 2, 2, TOK], F32R)
        v_both = sb("v_both", [P, 2, TT, 4, 2 * HD], F32R)
        probs = sb("probs", [P, 4, QT * SEQ])
        neg_max = sb("neg_max", [P, 4 * QT])
        row_sum = sb("row_sum", [P, 4 * QT])
        row_inv = sb("row_inv", [P, 4 * QT])
        pt_hi, pt_lo = (sb(f"probsT_{n}", [P, 2, KT * SEQ], F32R) for n in ("hi", "lo"))
        o_part = sb("o_part", [P, SEQ])
        o_sum = sb("o_sum", [P, SEQ])
        o_hi, o_lo = (sb(f"oT_{n}", [P, 2, TOK], F32R) for n in ("hi", "lo"))
        y_t = sb("y_t", [P, XT, TOK])
        neg_bias = sb("neg_bias", [P, LAYERS, QT, SEQ])
        identity = sb("identity", [P, P])
        bo_col = sb("bo_col", [P, LAYERS * XT])
        mask_col = sb("mask_col", [P, 2 * QT])
        mask_term = sb("mask_term", [P, 2 * QT])
        index_int = sb("index_int", [P, LAYERS * 4], I32)
        index_f = sb("index_f", [P, LAYERS * 4])
        index_wrap = sb("index_wrap", [P, LAYERS * 4])
        bias_part = sb("bias_part", [P, SEQ])

        def flat(ap):
            return ap.rearrange("p a b -> p (a b)")

        y_rows = x_raw[:, :].rearrange("p (t c) -> p t c", t=TT)
        stage = {"P0": flat(probs[:, 0:2, :]), "P1": flat(probs[:, 2:4, :]), "Y": flat(y_t[:, :, :]),
                 "C0": flat(ctx_raw[:, 0:2, :]), "C1": flat(ctx_raw[:, 2:4, :]), "X": x_raw[:, :]}

        def chunk(w, i):
            kind, t = CHUNKS[i]
            return w[kind][:, t, :] if kind != "o" else flat(w[kind][:, 4 * t:4 * t + 4, :])

        job_bank = [bank(f"job_bank{i}") for i in range(2)]
        s_bank = [bank(f"s_bank{i}") for i in range(2)]
        pt_bank = bank("pt_bank")
        o_bank = bank("o_bank")
        y_bank = [bank(f"y_bank{i}") for i in range(XT)]

        x_mid = nc.dram_tensor("x_mid", [GROUPS, P, XT * TOK], F32, kind="Internal").ap()

        dve_seen = sem("dve_seen")
        pool_seen = sem("pool_seen")
        small_in = per_layer("small_in")
        bias_steps = per_layer("bias_steps")
        pool_setup = sem("pool_setup")
        w_in = [{s: sem(f"w_in{s}_{n}") for s in sorted(set(STAGES[n]))} for n in range(LAYERS)]
        w_hi_done = per_layer("w_hi_done")
        w_lo_done = per_layer("w_lo_done")
        ctx_in = per_layer("ctx_in")
        x_in = per_layer("x_in")
        x_split = per_layer("x_split")
        job_mm = per_layer("job_mm")
        job_hi = per_layer("job_hi")
        job_lo = per_layer("job_lo")
        k_dup_done = per_layer("k_dup_done")
        s_done = per_layer("s_done")
        logits = per_layer("logits")
        exps = per_layer("exps")
        inverse = per_layer("inverse")
        normal = per_layer("normal")
        pt_mm = per_layer("pt_mm")
        pt_hi_done = per_layer("pt_hi_done")
        pt_lo_done = per_layer("pt_lo_done")
        pv_done = per_layer("pv_done")
        o_part_done = per_layer("o_part_done")
        o_sum_done = per_layer("o_sum_done")
        o_hi_done = per_layer("o_hi_done")
        o_lo_done = per_layer("o_lo_done")
        y_mm = per_layer("y_mm")
        y_init = per_layer("y_init")
        y_done = per_layer("y_done")
        y_out = per_layer("y_out")

        def wait(engine, semaphore, value):
            if not isinstance(value, int) or value > 0:
                engine.wait_ge(semaphore, value)

        def load_columns(engine, landed, to, vectors):
            tiles = [v[t * P:(t + 1) * P] for v in vectors for t in range(v.shape[0] // P)]
            for i, tile in enumerate(tiles):
                engine.dma_start(to[:, i:i + 1], tile.rearrange("(p a) -> p a", a=1)).then_inc(landed, 16)

        def load_indices(engine, n):
            for i in range(2):
                engine.dma_start(index_int[:, 4 * n + 2 * i:4 * n + 2 * i + 2],
                                 weights[n][5 + i].partition_broadcast(P)).then_inc(small_in[n], 16)

        def make_bias(engine, n, part_a, part_b):
            steps = 0

            def step(instruction):
                nonlocal steps
                steps += 1
                instruction.then_inc(bias_steps[n], 1)
                engine.wait_ge(bias_steps[n], steps)

            index = index_f[:, 4 * n:4 * n + 4]
            wrap = index_wrap[:, 4 * n:4 * n + 4]
            step(engine.tensor_copy(index, index_int[:, 4 * n:4 * n + 4]))
            step(engine.tensor_scalar(wrap, index, 0.0, float(SEQ), ALU.is_lt, ALU.mult))
            step(engine.tensor_tensor(index, index, wrap, ALU.add))
            is_a, is_b = neg_bias[:, n, 0, :], neg_bias[:, n, 1, :]
            for i, to in enumerate((is_a, is_b)):
                at = 4 * n + 2 * i
                step(engine.tensor_scalar(to, o_sum[:, :], index_f[:, at:at + 1], None, ALU.is_equal))
                step(engine.tensor_scalar(part_a, o_sum[:, :], index_f[:, at + 1:at + 2], None, ALU.is_equal))
                step(engine.tensor_tensor(to, part_a, to, ALU.add))
                step(engine.tensor_scalar(to, to, 1.0, None, ALU.min))
            assert steps == BIAS_FOUND
            step(engine.tensor_tensor(part_a, is_a, is_b, ALU.mult))
            step(engine.tensor_tensor(is_a, is_a, part_a, ALU.subtract))
            step(engine.tensor_scalar(part_a, is_a, mask_term[:, 0:1], None, ALU.mult))
            step(engine.tensor_scalar(part_b, is_b, mask_term[:, QT:QT + 1], None, ALU.mult))
            step(engine.tensor_tensor(part_a, part_a, part_b, ALU.add))
            step(engine.tensor_scalar(is_a, is_a, mask_term[:, 1:2], None, ALU.mult))
            step(engine.tensor_scalar(is_b, is_b, mask_term[:, QT + 1:QT + 2], None, ALU.mult))
            step(engine.tensor_tensor(is_b, is_b, is_a, ALU.add))
            step(engine.tensor_copy(is_a, part_a))
            assert steps == BIAS_STEPS

        LAST = GROUPS - 1
        plans = [plan(n) for n in range(LAYERS)]
        x_rows = x.rearrange("b s c -> (b s) c").rearrange("(g t p) c -> g p t c", t=TT, p=P)
        ctx_rows = ctx.rearrange("b s c -> (b s) c").rearrange("(g t p) c -> g p t c", t=TT, p=P)
        out_rows = out.rearrange("b s c -> (b s) c").rearrange("(g t p) c -> g p t c", t=TT, p=P)

        block = stack.enter_context(nc.Block())

        @block.sync
        def _(sp):
            for n in range(LAYERS):
                wq, wk, wv, wo, bo, at_a, at_b = weights[n]
                here = plans[n]
                rows = {"q": wq.rearrange("(t p) n -> t p n", p=P), "k": wk.rearrange("(t p) n -> t p n", p=P),
                        "v": wv.rearrange("(t p) n -> t p n", p=P), "o": wo.rearrange("(h j p) c -> h p j c", h=2, p=P)}

                def load_ctx(g):
                    sp.dma_start(ctx_raw[:, :, :], ctx_rows[g]).then_inc(ctx_in[n], 16)

                def load_x(g):
                    if n == 0:
                        sp.dma_start(x_raw[:, :].rearrange("p (t c) -> p t c", t=TT), x_rows[g]).then_inc(x_in[n], 16)
                    else:
                        sp.dma_start(x_raw[:, :], x_mid[g]).then_inc(x_in[n], 16)

                def load_chunk(i):
                    kind, t = CHUNKS[i]
                    if (before := chunk_before(n, i)) is not None:
                        sp.wait_ge(w_lo_done[n], before + 1)
                    to = stage[STAGES[n][i]]
                    if kind == "o":
                        to = to.rearrange("p (j c) -> p j c", j=PAIRS // 2)
                    sp.dma_start(to, rows[kind][t]).then_inc(w_in[n][STAGES[n][i]], 16)

                def store(g):
                    if n == 0:
                        sp.wait_ge(y_done[n], g * XT + XT)
                        sp.dma_start(x_mid[g], flat(y_t[:, :, :])).then_inc(y_out[n], 16)
                    else:
                        done = here["jobs in all"] if isinstance(g, int) and g == LAST else here["jobs before", UNITS + 2, True]
                        sp.wait_ge(job_lo[n], g * here["jobs of a group"] + done)
                        sp.dma_start(out_rows[g], y_rows).then_inc(y_out[n], 16)

                if n == 0:
                    load_ctx(0)
                    load_x(0)
                    for i in range(3):
                        load_chunk(i)
                    load_indices(sp, 1)
                    load_columns(sp, small_in[1], bo_col, [weights[m][4] for m in range(LAYERS)])
                    sp.wait_ge(job_mm[n], CT + XT)
                    for i in range(3, len(CHUNKS)):
                        load_chunk(i)
                else:
                    at = (LAST - 1) * plans[0]["jobs of a group"]
                    sp.wait_ge(job_mm[0], at + plans[0]["x turned"])
                    for i in range(K_Q_V_CHUNKS):
                        load_chunk(i)
                    sp.wait_ge(w_lo_done[n], K_Q_V_CHUNKS - 1)
                    sp.wait_ge(y_out[0], 16 * LAST)
                    load_x(0)
                    sp.wait_ge(w_lo_done[n], K_Q_V_CHUNKS)
                    load_ctx(0)
                    sp.wait_ge(y_done[0], GROUPS * XT)
                    sp.dma_start(x_mid[LAST], flat(y_t[:, :, :])).then_inc(y_out[0], 16)
                    sp.wait_ge(job_mm[n], CT)
                    sp.wait_ge(x_split[n], 2)
                    for i in range(K_Q_V_CHUNKS, len(CHUNKS)):
                        load_chunk(i)
                    sp.wait_ge(y_out[0], 16 * GROUPS)
                sp.wait_ge(w_lo_done[n], len(CHUNKS))
                load_ctx(1)
                load_x(1)
                with sp.Fori(0, LAST - 1) as g:
                    sp.wait_ge(job_mm[n], g * here["jobs of a group"] + here["ctx turned"])
                    load_ctx(g + 2)
                    if n == 0:
                        sp.wait_ge(job_mm[n], g * here["jobs of a group"] + here["x turned"])
                        load_x(g + 2)
                    store(g)
                    if n == 1:
                        sp.wait_ge(y_out[n], g * 16 + 16)
                        sp.wait_ge(x_split[n], g * 2 + 4)
                        load_x(g + 2)
                store(LAST - 1)

                if n == 1:
                    store(LAST)
                    sp.wait_ge(y_out[1], 16 * GROUPS)

        @block.gpsimd
        def _(pool):
            pool.iota(o_part[:, :].bitcast(I32), pattern=[[1, SEQ]], base=0, channel_multiplier=0).then_inc(pool_setup, 1)
            pool.memset(identity[:, :], 0.0).then_inc(pool_setup, 1)
            pool.wait_ge(pool_setup, 2)
            pool.affine_select(out=identity[:, :], in_=identity[:, :], compare_op=ALU.not_equal, fill=1.0,
                               base=0, pattern=[[-1, P]], channel_multiplier=1).then_inc(pool_setup, 1)
            for e in range(2):
                other = slice((1 - e) * HD, (2 - e) * HD)
                pool.wait_ge(pool_setup, 3 + e)
                pool.memset(k_low[other, :, e, :].bitcast(F32), 0.0).then_inc(pool_setup, 1)

            pool.wait_ge(small_in[0], 16 * (2 * QT + 2))
            pool.wait_ge(pool_setup, 5)
            pool.tensor_copy(o_sum[:, :], o_part[:, :].bitcast(I32)).then_inc(pool_setup, 1)
            pool.tensor_scalar(mask_term[:, :], mask_col[:, :], -1.0, 1.0, ALU.mult, ALU.add).then_inc(pool_setup, 1)
            pool.wait_ge(pool_setup, 7)
            pool.tensor_scalar(mask_term[:, :], mask_term[:, :], SUPPRESS, None, ALU.mult).then_inc(pool_setup, 1)
            pool.wait_ge(pool_setup, 8)
            make_bias(pool, 0, o_part[:, :], bias_part[:, :])

            for n in range(LAYERS):
                here = plans[n]

                def split_output(g, u):
                    to, pair = slice(u % GB * SEQ, (u % GB + 1) * SEQ), u // GB
                    if u % GB == 0 and pair >= 2:
                        pool.wait_ge(y_mm[n], g * PAIRS + pair - 1)
                        pool.sem_inc(pool_seen, 1)
                    pool.wait_ge(o_sum_done[n], g * 2 * UNITS + 2 * u + 2)
                    pool.sem_inc(pool_seen, 1)
                    pool.tensor_scalar(o_hi[:, pair % 2, to], o_sum[:, :], 1.0, 1.0, ALU.mult, ALU.mult).then_inc(o_hi_done[n], 1)
                    pool.wait_ge(o_hi_done[n], g * UNITS + u + 1)
                    pool.tensor_tensor(o_lo[:, pair % 2, to], o_sum[:, :], o_hi[:, pair % 2, to].bitcast(F32),
                                       ALU.subtract).then_inc(o_lo_done[n], 1)

                def normalise(g, h):
                    pool.wait_ge(inverse[n], g * 2 * UNITS + h + 1)
                    pool.sem_inc(pool_seen, 1)
                    for t in range(QT):
                        i = h % 4 * QT + t
                        at = probs[:, h % 4, t * SEQ:(t + 1) * SEQ]
                        last = pool.tensor_scalar(at, at, row_inv[:, i:i + 1], 1.0, ALU.mult, ALU.mult)
                    last.then_inc(normal[n], 1)

                def split_x(g):
                    pool.wait_ge(x_split[n], g * 2 + 1)
                    pool.tensor_tensor(flat(x_lo[:, :, :]), x_raw[:, :], flat(x_hi[:, :, :]).bitcast(F32),
                                      ALU.subtract).then_inc(x_split[n], 1)

                def duplicate(g, pair, place):
                    for index, kind, i, _, _ in place:
                        if kind == "k":
                            pool.wait_ge(job_hi[n], g * here["jobs of a group"] + index + 1)
                            pool.sem_inc(pool_seen, 1)
                            for e in range(2):
                                own, other = slice(e * HD, (e + 1) * HD), slice((1 - e) * HD, (2 - e) * HD)
                                pool.tensor_scalar(k_dup[other, i % 2, e, :], k_dup[own, i % 2, e, :].bitcast(F32),
                                                   1.0, 1.0, ALU.mult, ALU.mult).then_inc(k_dup_done[n], 1)
                                pool.wait_ge(k_dup_done[n], g * 2 * PAIRS + 2 * pair + e + 1)
                                pool.sem_inc(pool_seen, 1)

                def slot(g, u, more=True):
                    if u == 13 and more and n == 1:
                        split_x(g + 1)
                    if u > 0:
                        split_output(g, u - 1)
                    if u + 1 < UNITS or more:
                        normalise(g, 2 * u + 2)
                        normalise(g, 2 * u + 3)
                    for place in here[u, more]:
                        if any(job[1] == "k" for job in place):
                            pool.wait_ge(normal[n], g * 2 * UNITS + 2 * u + 4)
                            duplicate(g, u // GB + 2, place)

                if n == 1:
                    split_x(0)
                    pool.wait_ge(x_split[n], 2)
                duplicate(0, 0, here["before"][:-1])
                for h in (0, 1):
                    normalise(0, h)
                pool.wait_ge(normal[n], 2)
                duplicate(0, 1, here["before"][-1:])
                for u in range(2):
                    slot(0, u)
                with nc.Fori(0, LAST, engines=(POOL,), hint_back_edge=True) as g:
                    for u in range(2, UNITS + 2):
                        slot(g, u)
                for u in range(2, UNITS):
                    slot(LAST, u, more=False)
                split_output(LAST, UNITS - 1)

        @block.tensor
        def _(pe):
            pe.wait_ge(pool_setup, 5)
            for n in range(LAYERS):
                here = plans[n]

                def product(to, left, right, first, last):
                    pe.matmul(to, left[0], right[0], start=first, stop=False)
                    pe.matmul(to, left[0], right[1], start=False, stop=False)
                    return pe.matmul(to, left[1], right[0], start=False, stop=last)

                def jobs(g, place):
                    for index, kind, i, t, ready in place:
                        bank = job_bank[index % 2]
                        wait(pe, job_lo[n], g * here["jobs of a group"] + ready)
                        cols = slice(i * P, (i + 1) * P)
                        if kind == "q":
                            for c in range(XT):
                                mm = product(bank[:, :], (w_hi["q"][:, c, cols], w_lo["q"][:, c, cols]),
                                             (x_hi[:, c, :], x_lo[:, c, :]), c == 0, c == XT - 1)
                        elif kind == "k":
                            for c in range(CT):
                                mm = product(bank[:, :], (w_hi["k"][:, c, cols], w_lo["k"][:, c, cols]),
                                             (ctx_hi[:, c, :], ctx_lo[:, c, :]), c == 0, c == CT - 1)
                        elif kind == "v":
                            rows, cols = slice(t * P, (t + 1) * P), slice(i * 4 * HD, (i + 1) * 4 * HD)
                            for c in range(CT):
                                mm = product(bank[:, 0:4 * HD], (ctx_hi[:, c, rows], ctx_lo[:, c, rows]),
                                             (w_hi["v"][:, c, cols], w_lo["v"][:, c, cols]), c == 0, c == CT - 1)
                        elif kind == "ctx":
                            for r in range(TT):
                                mm = pe.transpose(bank[:, r * P:(r + 1) * P], ctx_raw[:, r, cols], identity[:, :])
                        elif kind == "x":
                            for r in range(TT):
                                at = r * CH + i * P
                                mm = pe.transpose(bank[:, r * P:(r + 1) * P], x_raw[:, at:at + P], identity[:, :])
                        else:
                            for r in (2 * i, 2 * i + 1):
                                for c in range(XT):
                                    at = (r % 2) * CH + c * P
                                    mm = pe.transpose(bank[:, at:at + P], y_t[:, c, r * P:(r + 1) * P], identity[:, :])
                        mm.then_inc(job_mm[n], 1)

                def scores(g, u):
                    wait(pe, logits[n], g * 4 * UNITS + 4 * u)
                    if u % GB == 0:
                        pe.wait_ge(k_dup_done[n], g * 2 * PAIRS + u // GB * 2 + 2)
                    pair, b = u // GB % 2, u % GB
                    for e in range(2):
                        for t in range(QT):
                            q = q_both[:, pair, e, b * SEQ + t * P:b * SEQ + (t + 1) * P]
                            to = s_bank[e][:, t * SEQ:(t + 1) * SEQ]
                            pe.matmul(to, q, k_dup[:, pair, e, b * SEQ:(b + 1) * SEQ], start=True, stop=False)
                            mm = pe.matmul(to, q, k_low[:, pair, e, b * SEQ:(b + 1) * SEQ], start=False, stop=True)
                    mm.then_inc(s_done[n], 1)

                def turn(g, h):
                    pe.wait_ge(normal[n], g * 2 * UNITS + h + 1)
                    wait(pe, pt_lo_done[n], g * 2 * UNITS + h)
                    for c in range(KT):
                        for t in range(QT):
                            mm = pe.transpose(pt_bank[:, c * SEQ + t * P:c * SEQ + (t + 1) * P],
                                              probs[:, h % 4, t * SEQ + c * P:t * SEQ + (c + 1) * P], identity[:, :])
                    mm.then_inc(pt_mm[n], 1)

                def times_v(g, u, e):
                    h = 2 * u + e
                    pe.wait_ge(pt_lo_done[n], g * 2 * UNITS + h + 1)
                    if e == 0:
                        wait(pe, o_sum_done[n], g * 2 * UNITS + 2 * u)
                    for c in range(KT):
                        v = v_both[:, u // 4 % 2, u % GB * KT + c, u // GB % 2 * 2 + e, :]
                        for part, first, last in ((pt_hi, c == 0, False), (pt_lo, False, c == KT - 1)):
                            mm = pe.matmul(o_bank[:, e * SEQ:(e + 1) * SEQ], v, part[:, h % 2, c * SEQ:(c + 1) * SEQ],
                                           start=first, stop=last)
                    mm.then_inc(pv_done[n], 1)

                def project_out(g, pair):
                    pe.wait_ge(o_lo_done[n], g * UNITS + 2 * pair + 2)
                    for c in range(XT):
                        cols = slice(c * P, (c + 1) * P)
                        mm = product(y_bank[c][:, :], (w_hi["o"][:, pair, cols], w_lo["o"][:, pair, cols]),
                                     (o_hi[:, pair % 2, :], o_lo[:, pair % 2, :]), pair == 0, pair == PAIRS - 1)
                    mm.then_inc(y_mm[n], 1)

                def slot(g, u, more=True):
                    places = here[u, more]
                    if u + 1 < UNITS or more:
                        if u % 2 == 1:
                            index = max(j[0] for place in here[u - 1, more] for j in place if j[1] == "q")
                            pe.wait_ge(job_lo[n], g * here["jobs of a group"] + index + 1)
                        scores(g, u + 1)
                    if u == 12 and more:
                        pe.wait_ge(ctx_in[n], g * 16 + 32)
                    if u == 13 and more and n == 0:
                        pe.wait_ge(x_in[n], g * 16 + 32)
                    if u == UNITS + 1 and n == 1:
                        pe.wait_ge(y_done[n], g * XT + XT)
                    jobs(g, places[0])
                    turn(g, 2 * u)
                    if u == 14 and more and n == 1:
                        pe.wait_ge(x_split[n], g * 2 + 4)
                    jobs(g, places[1])
                    turn(g, 2 * u + 1)
                    pe.wait_ge(job_lo[n], g * here["jobs of a group"] + here["jobs before", u, more])
                    times_v(g, u, 0)
                    jobs(g, places[2])
                    if u % 2 == 0 and u > 0:
                        project_out(g, u // GB - 1)
                    jobs(g, places[3])
                    times_v(g, u, 1)
                    if u == UNITS + 1:
                        pe.wait_ge(y_done[n], g * XT + XT)

                pe.wait_ge(ctx_in[n], 16)
                if n == 0:
                    pe.wait_ge(x_in[n], 16)
                jobs(0, here["before"][:-3])
                pe.wait_ge(w_lo_done[n], K_Q_CHUNKS)
                if n == 1:
                    pe.wait_ge(x_split[n], 2)
                jobs(0, here["before"][-3:])
                pe.wait_ge(job_lo[n], len(here["before"]) - 1)
                scores(0, 0)
                pe.wait_ge(w_lo_done[n], K_Q_V_CHUNKS)
                jobs(0, here["behind"])
                for u in range(2):
                    slot(0, u)
                pe.wait_ge(w_lo_done[n], len(CHUNKS))
                with nc.Fori(0, LAST, engines=(PE,), hint_back_edge=True) as g:
                    for u in range(2, UNITS + 2):
                        slot(g, u)
                for u in range(2, UNITS):
                    slot(LAST, u, more=False)
                project_out(LAST, PAIRS - 1)
                if n == 1:
                    pe.wait_ge(y_done[n], GROUPS * XT)
                    jobs(LAST, here["end"])

        @block.scalar
        def _(act):
            load_indices(act, 0)
            load_columns(act, small_in[0], mask_col, (mask_a, mask_b))

            def split_chunk(n, i):
                loads = STAGES[n][:i + 1].count(STAGES[n][i])
                act.wait_ge(w_in[n][STAGES[n][i]], 16 * loads)
                act.activation(chunk(w_hi, i), stage[STAGES[n][i]], ACT.Copy).then_inc(w_hi_done[n], 1)

            for n in range(LAYERS):
                here = plans[n]

                def high(g, place):
                    for index, kind, i, t, _ in place:
                        bank = job_bank[index % 2]
                        act.wait_ge(job_mm[n], g * here["jobs of a group"] + index + 1)
                        if kind == "q":
                            for e in range(2):
                                own = slice(e * HD, (e + 1) * HD)
                                ins = act.activation(q_both[own, i % 2, e, :], bank[own, :], ACT.Copy, scale=-SCALE)
                        elif kind == "k":
                            for e in range(2):
                                own = slice(e * HD, (e + 1) * HD)
                                ins = act.activation(k_dup[own, i % 2, e, :], bank[own, :], ACT.Copy)
                        elif kind == "v":
                            ins = act.activation(v_both[:, i % 2, t, :, 0:HD],
                                                 bank[:, 0:4 * HD].rearrange("p (h d) -> p h d", h=4), ACT.Copy)
                        elif kind == "ctx":
                            ins = act.activation(ctx_hi[:, i, :], bank[:, :], ACT.Copy)
                        elif kind == "x":
                            ins = act.activation(x_hi[:, i, :], bank[:, :], ACT.Copy)
                        else:
                            ins = act.activation(y_rows[:, 2 * i, :], bank[:, 0:CH], ACT.Copy)
                        ins.then_inc(job_hi[n], 1)

                def split_x(g):
                    act.wait_ge(x_in[n], g * 16 + 16)
                    act.activation(flat(x_hi[:, :, :]), x_raw[:, :], ACT.Copy).then_inc(x_split[n], 1)

                def exponential(g, h):
                    for t in range(QT):
                        act.wait_ge(logits[n], g * 4 * UNITS + 2 * h + t + 1)
                        i = h % 4 * QT + t
                        at = probs[:, h % 4, t * SEQ:(t + 1) * SEQ]
                        act.activation(at, at, ACT.Exp, bias=neg_max[:, i:i + 1], scale=-1.0,
                                       accum_out=row_sum[:, i:i + 1]).then_inc(exps[n], 1)

                def probs_high(g, h):
                    act.wait_ge(pt_mm[n], g * 2 * UNITS + h + 1)
                    act.activation(pt_hi[:, h % 2, :], pt_bank[:, :], ACT.Copy).then_inc(pt_hi_done[n], 1)

                def move_parts(g, u):
                    act.wait_ge(pv_done[n], g * 2 * UNITS + 2 * u + 2)
                    act.activation(o_part[0:HD, :], o_bank[HD:P, 0:SEQ], ACT.Copy).then_inc(o_part_done[n], 1)
                    act.activation(o_part[HD:P, :], o_bank[0:HD, SEQ:2 * SEQ], ACT.Copy).then_inc(o_part_done[n], 1)

                def slot(g, u, more=True):
                    places = here[u, more]
                    split_here = SPLIT_IN_SLOT.get(u, ()) if n == 0 and not more else ()
                    if u > 0:
                        move_parts(g, u - 1)
                    high(g, places[0])
                    probs_high(g, 2 * u)
                    if u + 1 < UNITS or more:
                        exponential(g, 2 * u + 2)
                    for i in split_here[:1]:
                        split_chunk(1, i)
                    if only_k(places[1]):
                        if u + 1 < UNITS or more:
                            exponential(g, 2 * u + 3)
                        probs_high(g, 2 * u + 1)
                        high(g, places[1])
                    else:
                        high(g, places[1][:1])
                        probs_high(g, 2 * u + 1)
                        high(g, places[1][1:])
                        if u + 1 < UNITS or more:
                            exponential(g, 2 * u + 3)
                    high(g, places[2])
                    high(g, places[3])
                    if u == 12 and more and n == 1:
                        act.wait_ge(y_init[n], g * XT + XT)
                        split_x(g + 1)
                    for i in split_here[1:]:
                        split_chunk(1, i)

                if n == 1:
                    act.wait_ge(y_init[0], GROUPS * XT)
                    split_x(0)
                high(0, here["before"][:-3])
                if n == 0:
                    for i in range(K_Q_CHUNKS):
                        split_chunk(0, i)
                high(0, here["before"][-3:-1])
                if n == 0:
                    for i in range(K_Q_CHUNKS, K_Q_V_CHUNKS):
                        split_chunk(0, i)
                high(0, here["before"][-1:])
                for h in (0, 1):
                    exponential(0, h)
                high(0, here["behind"])
                if n == 1:
                    act.wait_ge(y_mm[0], GROUPS * PAIRS)
                for i in range(K_Q_V_CHUNKS, len(CHUNKS)):
                    split_chunk(n, i)
                for u in range(2):
                    slot(0, u)
                with nc.Fori(0, LAST, engines=(ACTIVATION,), hint_back_edge=True) as g:
                    for u in range(2, UNITS + 2):
                        slot(g, u)
                for u in range(2, UNITS):
                    slot(LAST, u, more=False)
                move_parts(LAST, UNITS - 1)
                if n == 1:
                    act.wait_ge(y_out[n], 16 * LAST)
                high(LAST, here["end"])

        @block.vector
        def _(dve):
            def split_chunk(n, i):
                dve.wait_ge(w_hi_done[n], i + 1)
                dve.tensor_tensor(chunk(w_lo, i), stage[STAGES[n][i]], chunk(w_hi, i).bitcast(F32),
                                  ALU.subtract).then_inc(w_lo_done[n], 1)

            for n in range(LAYERS):
                here = plans[n]

                def low(g, place):
                    for index, kind, i, t, _ in place:
                        bank = job_bank[index % 2]
                        dve.wait_ge(job_hi[n], g * here["jobs of a group"] + index + 1)
                        if kind == "q":
                            for e in range(2):
                                own, other = slice(e * HD, (e + 1) * HD), slice((1 - e) * HD, (2 - e) * HD)
                                ins = dve.scalar_tensor_tensor(out=q_both[other, i % 2, e, :], in0=bank[own, :], scalar=-SCALE,
                                                               in1=q_both[own, i % 2, e, :].bitcast(F32),
                                                               op0=ALU.mult, op1=ALU.subtract)
                        elif kind == "k":
                            for e in range(2):
                                own = slice(e * HD, (e + 1) * HD)
                                ins = dve.tensor_tensor(k_low[own, i % 2, e, :], bank[own, :],
                                                        k_dup[own, i % 2, e, :].bitcast(F32), ALU.subtract)
                        elif kind == "v":
                            ins = dve.tensor_tensor(v_both[:, i % 2, t, :, HD:2 * HD],
                                                    bank[:, 0:4 * HD].rearrange("p (h d) -> p h d", h=4),
                                                    v_both[:, i % 2, t, :, 0:HD].bitcast(F32), ALU.subtract)
                        elif kind == "ctx":
                            ins = dve.tensor_tensor(ctx_lo[:, i, :], bank[:, :], ctx_hi[:, i, :].bitcast(F32), ALU.subtract)
                        elif kind == "x":
                            ins = dve.tensor_tensor(x_lo[:, i, :], bank[:, :], x_hi[:, i, :].bitcast(F32), ALU.subtract)
                        else:
                            ins = dve.tensor_copy(y_rows[:, 2 * i + 1, :], bank[:, CH:2 * CH])
                        ins.then_inc(job_lo[n], 1)

                def begin_y(g, c):
                    dve.scalar_tensor_tensor(out=y_t[:, c, :], in0=x_hi[:, c, :].bitcast(F32),
                                             scalar=bo_col[:, n * XT + c:n * XT + c + 1],
                                             in1=x_lo[:, c, :].bitcast(F32), op0=ALU.add, op1=ALU.add).then_inc(y_init[n], 1)

                def end_y(g):
                    dve.wait_ge(y_mm[n], g * PAIRS + PAIRS)
                    dve.wait_ge(y_init[n], g * XT + XT)
                    for c in range(XT):
                        dve.tensor_tensor(y_t[:, c, :], y_bank[c][:, :], y_t[:, c, :], ALU.add).then_inc(y_done[n], 1)

                def logit(g, h):
                    dve.wait_ge(s_done[n], g * UNITS + h // 2 + 1)
                    dve.sem_inc(dve_seen, 1)
                    for t in range(QT):
                        i = h % 4 * QT + t
                        dve.tensor_tensor_reduce(out=probs[:, h % 4, t * SEQ:(t + 1) * SEQ],
                                                 in0=s_bank[h % 2][:, t * SEQ:(t + 1) * SEQ], in1=neg_bias[:, n, t, :],
                                                 scale=1.0, scalar=FMAX, op0=ALU.add, op1=ALU.min,
                                                 accum_out=neg_max[:, i:i + 1]).then_inc(logits[n], 1)

                def invert(g, h):
                    dve.wait_ge(exps[n], g * 4 * UNITS + 2 * h + 2)
                    i = h % 4 * QT
                    dve.reciprocal(row_inv[:, i:i + QT], row_sum[:, i:i + QT]).then_inc(inverse[n], 1)

                def probs_low(g, h):
                    dve.wait_ge(pt_hi_done[n], g * 2 * UNITS + h + 1)
                    dve.tensor_tensor(pt_lo[:, h % 2, :], pt_bank[:, :], pt_hi[:, h % 2, :].bitcast(F32),
                                      ALU.subtract).then_inc(pt_lo_done[n], 1)

                def sum_parts(g, u):
                    dve.wait_ge(o_part_done[n], g * 2 * UNITS + 2 * u + 2)
                    wait(dve, o_lo_done[n], g * UNITS + u)
                    for e in range(2):
                        rows = slice(e * HD, (e + 1) * HD)
                        dve.tensor_tensor(o_sum[rows, :], o_bank[rows, e * SEQ:(e + 1) * SEQ], o_part[rows, :],
                                          ALU.add).then_inc(o_sum_done[n], 1)

                def slot(g, u, more=True):
                    places = here[u, more]
                    split_here = SPLIT_IN_SLOT.get(u, ()) if n == 0 and not more else ()
                    if u + 1 < UNITS or more:
                        logit(g, 2 * u + 2)
                    if u % 2 == 1:
                        low(g, places[0])
                    if u > 0:
                        sum_parts(g, u - 1)
                    if u % 2 == 0:
                        low(g, places[0])
                    probs_low(g, 2 * u)
                    if u + 1 < UNITS or more:
                        logit(g, 2 * u + 3)
                        invert(g, 2 * u + 2)
                    for i in split_here[:1]:
                        split_chunk(1, i)
                    if only_k(places[1]):
                        if u + 1 < UNITS or more:
                            invert(g, 2 * u + 3)
                        probs_low(g, 2 * u + 1)
                        low(g, places[1])
                    else:
                        early = 2 if u == 12 else 1
                        low(g, places[1][:early])
                        probs_low(g, 2 * u + 1)
                        low(g, places[1][early:])
                        if u + 1 < UNITS or more:
                            invert(g, 2 * u + 3)
                    low(g, places[2] + places[3])
                    if u == UNITS:
                        end_y(g)
                    if u == UNITS + 1 and n == 0:
                        dve.wait_ge(y_out[n], g * 16 + 16)
                    if u in (4, 6):
                        begin_y(g, u // 2 - 2)
                    for i in split_here[1:]:
                        split_chunk(1, i)

                low(0, here["before"][:-3])
                if n == 0:
                    for i in range(K_Q_CHUNKS):
                        split_chunk(0, i)
                    dve.wait_ge(small_in[1], 16 * (2 + XT * LAYERS))
                    dve.wait_ge(pool_setup, 8)
                    dve.wait_ge(bias_steps[0], BIAS_FOUND)
                    make_bias(dve, 1, pt_bank[:, 0:SEQ], o_sum[:, :])
                low(0, here["before"][-3:-1])
                if n == 0:
                    for i in range(K_Q_CHUNKS, K_Q_V_CHUNKS):
                        split_chunk(0, i)
                low(0, here["before"][-1:])
                if n == 0:
                    dve.wait_ge(w_lo_done[n], K_Q_V_CHUNKS)
                    dve.wait_ge(bias_steps[0], BIAS_STEPS)
                for h in (0, 1):
                    logit(0, h)
                for h in (0, 1):
                    invert(0, h)
                low(0, here["behind"])
                for i in range(K_Q_V_CHUNKS, len(CHUNKS)):
                    split_chunk(n, i)
                for u in range(2):
                    slot(0, u)
                if n == 1:
                    dve.wait_ge(y_out[0], 16 * GROUPS)
                with nc.Fori(0, LAST, engines=(VECTOR,), hint_back_edge=True) as g:
                    for u in range(2, UNITS + 2):
                        slot(g, u)
                for u in range(2, UNITS):
                    slot(LAST, u, more=False)
                sum_parts(LAST, UNITS - 1)
                end_y(LAST)
                if n == 1:
                    dve.wait_ge(y_out[n], 16 * LAST)
                low(LAST, here["end"])


_INS = ["x", "ctx_2048", "mask_S_fk1", "mask_S_fk0"] + [
    f"L{n}_xattn_{w}" for n in range(LAYERS)
    for w in ("Wq", "Wk", "Wv", "Wo", "bo", "token_indices_A", "token_indices_B")]


def kernel(**inputs):
    import numpy as _np
    import concourse.bacc as _bacc
    from concourse import mybir as _mybir
    from concourse.bass_utils import run_bass_kernel_spmd as _run

    nc = _bacc.Bacc("TRN2", target_bir_lowering=False, num_devices=1)
    arrays, args = {}, {}
    for name in _INS:
        a = _np.ascontiguousarray(inputs[name])
        arrays[f"in_{name}_dram"] = a
        args[name] = nc.dram_tensor(f"in_{name}_dram", a.shape, _mybir.dt.from_np(a.dtype), kind="ExternalInput").ap()
    out = nc.dram_tensor("out_0_dram", inputs["x"].shape, _mybir.dt.from_np(_np.dtype("float32")), kind="ExternalOutput").ap()
    weights = [[args[f"L{n}_xattn_{w}"] for w in ("Wq", "Wk", "Wv", "Wo", "bo", "token_indices_A", "token_indices_B")]
               for n in range(LAYERS)]
    two_layers_of_cross_attention(nc, args["x"], args["ctx_2048"], args["mask_S_fk1"], args["mask_S_fk0"], weights, out)
    r = _run(nc, [arrays], core_ids=[0])
    return r.results[0]["out_0_dram"]
```
